# Optimizing a Trainium2 kernel written in Bass

```python
import numpy as np
import jax
import jax.numpy as jnp

def _softmax(x, axis=-1):
    return jax.nn.softmax(x, axis=axis)

def _gelu(x):
    return jax.nn.gelu(x, approximate=True)

def _silu(x):
    return jax.nn.silu(x)

def _sigmoid(x):
    return jax.nn.sigmoid(x)

def _layernorm(x, axis=-1, eps=1e-05):
    m = jnp.mean(x, axis=axis, keepdims=True)
    v = jnp.var(x, axis=axis, keepdims=True)
    return (x - m) / jnp.sqrt(v + eps)

def _scatter_add(tgt, idx, src, axis=0):
    return tgt.at[idx].add(src)

def _segment_sum(src, seg, n):
    return jax.ops.segment_sum(src, seg, n)
kernel_name = 'mk_seq_postln_d2_jaxref_r8_e1b290'

def setup_inputs(seed: int=0):
    np.random.seed(seed)
    _w = jnp.asarray

    def _L0_attn_setup():
        import math
        import jax, jax.numpy as jnp
        import numpy as np
        D_MODEL = 128
        N_HEADS = 16
        D_K = D_MODEL // N_HEADS
        THETA = 10000.0

        def _rope(t, cos, sin):
            B, H, S, d = t.shape
            tp = t.reshape(B, H, S, d // 2, 2)
            even, odd = (tp[..., 0], tp[..., 1])
            r_even = even * cos - odd * sin
            r_odd = even * sin + odd * cos
            return jnp.stack([r_even, r_odd], axis=-1).reshape(B, H, S, d)
        key = jax.random.key(seed)
        k1, k2, k3 = jax.random.split(key, 3)
        B, S = (2, 256)
        x = jax.random.normal(k1, (B, S, D_MODEL), dtype=jnp.float32)
        std_qkv = math.sqrt(2.0 / (D_MODEL + 3 * D_MODEL))
        std_out = math.sqrt(2.0 / (D_MODEL + D_MODEL))
        w_qkv = jnp.clip(jax.random.normal(k2, (3 * D_MODEL, D_MODEL), dtype=jnp.float32) * std_qkv, -3 * std_qkv, 3 * std_qkv)
        b_qkv = jnp.zeros((3 * D_MODEL,), dtype=jnp.float32)
        w_out = jnp.clip(jax.random.normal(k3, (D_MODEL, D_MODEL), dtype=jnp.float32) * std_out, -3 * std_out, 3 * std_out)
        b_out = jnp.zeros((D_MODEL,), dtype=jnp.float32)
        return {'x': x, 'w_qkv': w_qkv, 'b_qkv': b_qkv, 'w_out': w_out, 'b_out': b_out}
    _L0_attn_in = _L0_attn_setup()

    def _L0_ffn_setup():
        import jax, jax.numpy as jnp
        import numpy as np
        DIM = 128
        DEPTH = 6
        HEADS = 16
        DIM_HEAD = 64
        WINDOW = 32
        INNER = HEADS * DIM_HEAD
        DIM_INNER = int(DIM * 4 * 2 / 3)
        QK_SCALE = 8.0

        def shift_tokens(t):
            a, s = jnp.split(t, 2, -1)
            s = jnp.pad(s, ((0, 0), (1, 0), (0, 0)))[:, :-1]
            return jnp.concatenate([a, s], -1)

        def l2norm(t):
            return t / jnp.maximum(jnp.linalg.norm(t, axis=-1, keepdims=True), 1e-12)

        def rotate_half(x):
            x1, x2 = jnp.split(x, 2, -1)
            return jnp.concatenate([-x2, x1], -1)

        def rotary_tables(n):
            half = jnp.arange(0, DIM_HEAD, 2, dtype=jnp.float32)
            inv_freq = 1.0 / 10000.0 ** (half / DIM_HEAD)
            t = jnp.arange(n, dtype=jnp.float32)
            freqs = t[:, None] * inv_freq[None, :]
            freqs = jnp.concatenate([freqs, freqs], -1)
            base_scale = (half + 0.4 * DIM_HEAD) / (1.4 * DIM_HEAD)
            power = (t - n // 2) / (WINDOW // 2)
            scale = base_scale[None, :] ** power[:, None]
            scale = jnp.concatenate([scale, scale], -1)
            return (freqs, scale)

        def local_attention(q, k, v):
            b, h, n, d = q.shape
            w = WINDOW
            nw = n // w
            bq = q.reshape(b, h, nw, w, d)
            bk = k.reshape(b, h, nw, w, d)
            bv = v.reshape(b, h, nw, w, d)

            def look(t):
                p = jnp.pad(t, ((0, 0), (0, 0), (1, 0), (0, 0), (0, 0)))
                return jnp.concatenate([p[:, :, :nw], p[:, :, 1:]], axis=3)
            bk2, bv2 = (look(bk), look(bv))
            seq = jnp.arange(n).reshape(nw, w)
            seq_p = jnp.pad(seq, ((1, 0), (0, 0)), constant_values=-1)
            jt = jnp.concatenate([seq_p[:nw], seq_p[1:]], axis=1)
            it = seq[:, :, None]
            jb = jt[:, None, :]
            mask = (it < jb) | (it > jb + w) | (jb == -1)
            sim = jnp.einsum('bhwie,bhwje->bhwij', bq, bk2) * QK_SCALE
            sim = jnp.where(mask, -jnp.finfo(sim.dtype).max, sim)
            attn = jax.nn.softmax(sim, -1)
            out = jnp.einsum('bhwij,bhwje->bhwie', attn, bv2)
            return out.reshape(b, h, n, d)

        def attn_layer(x, Wqkv, qs, ksc, Wo):
            b, n, _ = x.shape
            qkv = x @ Wqkv
            q, k, v = jnp.split(qkv, 3, -1)
            sh = lambda t: t.reshape(b, n, HEADS, DIM_HEAD).transpose(0, 2, 1, 3)
            q, k, v = (sh(q), sh(k), sh(v))
            q = l2norm(q) * qs
            k = l2norm(k) * ksc
            freqs, scale = rotary_tables(n)
            cos, sin = (jnp.cos(freqs), jnp.sin(freqs))
            q = q * cos * scale + rotate_half(q) * sin * scale
            inv = 1.0 / scale
            k = k * cos * inv + rotate_half(k) * sin * inv
            out = local_attention(q, k, v)
            out = out.transpose(0, 2, 1, 3).reshape(b, n, INNER)
            return out @ Wo

        def ffn_layer(x, g, bln, W1, b1, W2, b2):
            mu = x.mean(-1, keepdims=True)
            var = ((x - mu) ** 2).mean(-1, keepdims=True)
            xn = (x - mu) / jnp.sqrt(var + 1e-05) * g + bln
            hg = xn @ W1 + b1
            a, gate = jnp.split(hg, 2, -1)
            return a * jax.nn.gelu(gate, approximate=False) @ W2 + b2
        key = jax.random.key(seed)
        ks = jax.random.split(key, 8)
        B, N = (2, 256)
        init = lambda k, shape: jax.random.normal(k, shape, jnp.float32) * 0.02
        return {'x': jax.random.normal(ks[0], (B, N, DIM), jnp.float32), 'Wqkv': init(ks[1], (DEPTH, DIM, 3 * INNER)), 'q_scale': jnp.ones((DEPTH, DIM_HEAD), jnp.float32), 'k_scale': jnp.ones((DEPTH, DIM_HEAD), jnp.float32), 'Wo': init(ks[2], (DEPTH, INNER, DIM)), 'ln_g': jnp.ones((DEPTH, DIM), jnp.float32), 'ln_b': jnp.zeros((DEPTH, DIM), jnp.float32), 'W1': init(ks[3], (DEPTH, DIM, 2 * DIM_INNER)), 'b1': jnp.zeros((DEPTH, 2 * DIM_INNER), jnp.float32), 'W2': init(ks[4], (DEPTH, DIM_INNER, DIM)), 'b2': jnp.zeros((DEPTH, DIM), jnp.float32)}
    _L0_ffn_in = _L0_ffn_setup()

    def _L1_attn_setup():
        import jax, jax.numpy as jnp
        import numpy as np
        DIM = 128

        def _circ_conv(x, key):
            D = x.shape[-1]
            return jnp.fft.irfft(jnp.fft.rfft(x, axis=-1) * jnp.fft.rfft(key), n=D, axis=-1)

        def _circ_corr(x, key):
            D = x.shape[-1]
            return jnp.fft.irfft(jnp.fft.rfft(x, axis=-1) * jnp.conj(jnp.fft.rfft(key)), n=D, axis=-1)
        key = jax.random.key(seed)
        k0, k1, k2 = jax.random.split(key, 3)
        B, T, D = (4, 256, DIM)
        x = jax.random.normal(k0, (B, T, D), dtype=jnp.float32)
        bind_key = jax.random.normal(k1, (D,), dtype=jnp.float32) * 0.02
        unbind_key = jax.random.normal(k2, (D,), dtype=jnp.float32) * 0.02
        gate = jnp.ones((1,), dtype=jnp.float32)
        decay = jnp.asarray(0.9, dtype=jnp.float32)
        return {'x': x, 'bind_key': bind_key, 'unbind_key': unbind_key, 'gate': gate, 'decay': decay}
    _L1_attn_in = _L1_attn_setup()

    def _L1_ffn_setup():
        import jax, jax.numpy as jnp
        import numpy as np
        E = 8
        K = 2
        CF = 1.25
        key = jax.random.key(seed)
        kx, kr, kg, ku, kd = jax.random.split(key, 5)
        D, F = (128, 512)
        x = jax.random.normal(kx, (4, 256, D), dtype=jnp.float32)
        router_w = 0.02 * jax.random.normal(kr, (E, D), dtype=jnp.float32)
        wg = jax.random.normal(kg, (E, D, F), dtype=jnp.float32) / np.sqrt(D)
        wu = jax.random.normal(ku, (E, D, F), dtype=jnp.float32) / np.sqrt(D)
        wd = jax.random.normal(kd, (E, F, D), dtype=jnp.float32) / np.sqrt(F)
        return {'x': x, 'router_w': router_w, 'wg': wg, 'wu': wu, 'wd': wd}
    _L1_ffn_in = _L1_ffn_setup()
    _d = {'L0_attn_x': _L0_attn_in['x'], 'L0_attn_w_qkv': _L0_attn_in['w_qkv'], 'L0_attn_b_qkv': _L0_attn_in['b_qkv'], 'L0_attn_w_out': _L0_attn_in['w_out'], 'L0_attn_b_out': _L0_attn_in['b_out'], 'L0_ffn_Wqkv': _L0_ffn_in['Wqkv'], 'L0_ffn_q_scale': _L0_ffn_in['q_scale'], 'L0_ffn_k_scale': _L0_ffn_in['k_scale'], 'L0_ffn_Wo': _L0_ffn_in['Wo'], 'L0_ffn_ln_g': _L0_ffn_in['ln_g'], 'L0_ffn_ln_b': _L0_ffn_in['ln_b'], 'L0_ffn_W1': _L0_ffn_in['W1'], 'L0_ffn_b1': _L0_ffn_in['b1'], 'L0_ffn_W2': _L0_ffn_in['W2'], 'L0_ffn_b2': _L0_ffn_in['b2'], 'L1_attn_bind_key': _L1_attn_in['bind_key'], 'L1_attn_unbind_key': _L1_attn_in['unbind_key'], 'L1_attn_gate': _L1_attn_in['gate'], 'L1_attn_decay': _L1_attn_in['decay'], 'L1_ffn_router_w': _L1_ffn_in['router_w'], 'L1_ffn_wg': _L1_ffn_in['wg'], 'L1_ffn_wu': _L1_ffn_in['wu'], 'L1_ffn_wd': _L1_ffn_in['wd']}
    _x0 = _d['L0_attn_x']
    _d['L0_attn_x'] = jax.random.normal(jax.random.fold_in(jax.random.key(seed), 1), (2, 1024, 128), dtype=_x0.dtype)
    del _x0
    return _d

def reference(L0_attn_x, L0_attn_w_qkv, L0_attn_b_qkv, L0_attn_w_out, L0_attn_b_out, L0_ffn_Wqkv, L0_ffn_q_scale, L0_ffn_k_scale, L0_ffn_Wo, L0_ffn_ln_g, L0_ffn_ln_b, L0_ffn_W1, L0_ffn_b1, L0_ffn_W2, L0_ffn_b2, L1_attn_bind_key, L1_attn_unbind_key, L1_attn_gate, L1_attn_decay, L1_ffn_router_w, L1_ffn_wg, L1_ffn_wu, L1_ffn_wd):

    def _L0_attn_ref(x, w_qkv, b_qkv, w_out, b_out):
        import math
        import jax, jax.numpy as jnp
        import numpy as np
        D_MODEL = 128
        N_HEADS = 16
        D_K = D_MODEL // N_HEADS
        THETA = 10000.0

        def _rope(t, cos, sin):
            B, H, S, d = t.shape
            tp = t.reshape(B, H, S, d // 2, 2)
            even, odd = (tp[..., 0], tp[..., 1])
            r_even = even * cos - odd * sin
            r_odd = even * sin + odd * cos
            return jnp.stack([r_even, r_odd], axis=-1).reshape(B, H, S, d)
        B, S, _ = x.shape
        qkv = jnp.einsum('bsi,oi->bso', x, w_qkv) + b_qkv
        qkv = qkv.reshape(B, S, 3, N_HEADS, D_K).transpose(2, 0, 3, 1, 4)
        q, k, v = (qkv[0], qkv[1], qkv[2])
        inv_freq = THETA ** (-jnp.arange(0, D_K, 2, dtype=jnp.float32) / D_K)
        ang = jnp.arange(S, dtype=jnp.float32)[:, None] * inv_freq[None, :]
        cos, sin = (jnp.cos(ang), jnp.sin(ang))
        q = _rope(q, cos, sin)
        k = _rope(k, cos, sin)
        scale = 1.0 / math.sqrt(D_K)
        scores = jnp.einsum('bhqd,bhkd->bhqk', q.astype(jnp.float32), k.astype(jnp.float32)) * scale
        causal = jnp.tril(jnp.ones((S, S), dtype=bool))
        scores = jnp.where(causal, scores, jnp.finfo(jnp.float32).min)
        ex = jnp.exp(scores - jnp.max(scores, axis=-1, keepdims=True))
        attn = ex / (jnp.sum(ex, axis=-1, keepdims=True) + 1e-08)
        attn = attn.astype(v.dtype)
        o = jnp.einsum('bhqk,bhkd->bhqd', attn, v)
        o = o.transpose(0, 2, 1, 3).reshape(B, S, D_MODEL)
        out = jnp.einsum('bsi,oi->bso', o, w_out) + b_out
        return out

    def _L0_ffn_ref(x, Wqkv, q_scale, k_scale, Wo, ln_g, ln_b, W1, b1, W2, b2):
        import jax, jax.numpy as jnp
        import numpy as np
        DIM = 128
        DEPTH = 6
        HEADS = 16
        DIM_HEAD = 64
        WINDOW = 32
        INNER = HEADS * DIM_HEAD
        DIM_INNER = int(DIM * 4 * 2 / 3)
        QK_SCALE = 8.0

        def shift_tokens(t):
            a, s = jnp.split(t, 2, -1)
            s = jnp.pad(s, ((0, 0), (1, 0), (0, 0)))[:, :-1]
            return jnp.concatenate([a, s], -1)

        def l2norm(t):
            return t / jnp.maximum(jnp.linalg.norm(t, axis=-1, keepdims=True), 1e-12)

        def rotate_half(x):
            x1, x2 = jnp.split(x, 2, -1)
            return jnp.concatenate([-x2, x1], -1)

        def rotary_tables(n):
            half = jnp.arange(0, DIM_HEAD, 2, dtype=jnp.float32)
            inv_freq = 1.0 / 10000.0 ** (half / DIM_HEAD)
            t = jnp.arange(n, dtype=jnp.float32)
            freqs = t[:, None] * inv_freq[None, :]
            freqs = jnp.concatenate([freqs, freqs], -1)
            base_scale = (half + 0.4 * DIM_HEAD) / (1.4 * DIM_HEAD)
            power = (t - n // 2) / (WINDOW // 2)
            scale = base_scale[None, :] ** power[:, None]
            scale = jnp.concatenate([scale, scale], -1)
            return (freqs, scale)

        def local_attention(q, k, v):
            b, h, n, d = q.shape
            w = WINDOW
            nw = n // w
            bq = q.reshape(b, h, nw, w, d)
            bk = k.reshape(b, h, nw, w, d)
            bv = v.reshape(b, h, nw, w, d)

            def look(t):
                p = jnp.pad(t, ((0, 0), (0, 0), (1, 0), (0, 0), (0, 0)))
                return jnp.concatenate([p[:, :, :nw], p[:, :, 1:]], axis=3)
            bk2, bv2 = (look(bk), look(bv))
            seq = jnp.arange(n).reshape(nw, w)
            seq_p = jnp.pad(seq, ((1, 0), (0, 0)), constant_values=-1)
            jt = jnp.concatenate([seq_p[:nw], seq_p[1:]], axis=1)
            it = seq[:, :, None]
            jb = jt[:, None, :]
            mask = (it < jb) | (it > jb + w) | (jb == -1)
            sim = jnp.einsum('bhwie,bhwje->bhwij', bq, bk2) * QK_SCALE
            sim = jnp.where(mask, -jnp.finfo(sim.dtype).max, sim)
            attn = jax.nn.softmax(sim, -1)
            out = jnp.einsum('bhwij,bhwje->bhwie', attn, bv2)
            return out.reshape(b, h, n, d)

        def attn_layer(x, Wqkv, qs, ksc, Wo):
            b, n, _ = x.shape
            qkv = x @ Wqkv
            q, k, v = jnp.split(qkv, 3, -1)
            sh = lambda t: t.reshape(b, n, HEADS, DIM_HEAD).transpose(0, 2, 1, 3)
            q, k, v = (sh(q), sh(k), sh(v))
            q = l2norm(q) * qs
            k = l2norm(k) * ksc
            freqs, scale = rotary_tables(n)
            cos, sin = (jnp.cos(freqs), jnp.sin(freqs))
            q = q * cos * scale + rotate_half(q) * sin * scale
            inv = 1.0 / scale
            k = k * cos * inv + rotate_half(k) * sin * inv
            out = local_attention(q, k, v)
            out = out.transpose(0, 2, 1, 3).reshape(b, n, INNER)
            return out @ Wo

        def ffn_layer(x, g, bln, W1, b1, W2, b2):
            mu = x.mean(-1, keepdims=True)
            var = ((x - mu) ** 2).mean(-1, keepdims=True)
            xn = (x - mu) / jnp.sqrt(var + 1e-05) * g + bln
            hg = xn @ W1 + b1
            a, gate = jnp.split(hg, 2, -1)
            return a * jax.nn.gelu(gate, approximate=False) @ W2 + b2
        for i in range(DEPTH):
            x = attn_layer(shift_tokens(x), Wqkv[i], q_scale[i], k_scale[i], Wo[i]) + x
            x = ffn_layer(shift_tokens(x), ln_g[i], ln_b[i], W1[i], b1[i], W2[i], b2[i]) + x
        return x

    def _L1_attn_ref(x, bind_key, unbind_key, gate, decay):
        import jax, jax.numpy as jnp
        import numpy as np
        DIM = 128

        def _circ_conv(x, key):
            D = x.shape[-1]
            return jnp.fft.irfft(jnp.fft.rfft(x, axis=-1) * jnp.fft.rfft(key), n=D, axis=-1)

        def _circ_corr(x, key):
            D = x.shape[-1]
            return jnp.fft.irfft(jnp.fft.rfft(x, axis=-1) * jnp.conj(jnp.fft.rfft(key)), n=D, axis=-1)
        B, T, D = x.shape
        bound = _circ_conv(x, bind_key)
        d = jax.nn.sigmoid(decay)
        pos = jnp.arange(T, dtype=x.dtype)
        diff = pos[:, None] - pos[None, :]
        causal = diff >= 0
        decay_matrix = jnp.where(causal, d ** jnp.maximum(diff, 0.0), 0.0)
        hologram = jnp.einsum('ts,bsd->btd', decay_matrix, bound)
        retrieved = _circ_corr(hologram, unbind_key)
        return x + gate * retrieved

    def _L1_ffn_ref(x, router_w, wg, wu, wd):
        import jax, jax.numpy as jnp
        import numpy as np
        E = 8
        K = 2
        CF = 1.25
        B, L, D = x.shape
        xf = x.reshape(-1, D)
        N = xf.shape[0]
        capacity = max(1, int(CF * N / E))
        logits = xf @ router_w.T
        probs = jax.nn.softmax(logits, axis=-1)
        topw, topi = jax.lax.top_k(probs, K)
        topw = topw / (topw.sum(-1, keepdims=True) + 1e-06)
        fe = topi.reshape(-1)
        fw = topw.reshape(-1)
        ft = jnp.repeat(jnp.arange(N), K)
        order = jnp.lexsort((-fw, fe))
        se, sw, st = (fe[order], fw[order], ft[order])
        counts = jax.ops.segment_sum(jnp.ones_like(se), se, num_segments=E)
        starts = jnp.cumsum(counts) - counts
        rank = jnp.arange(N * K) - starts[se]
        keep = rank < capacity
        pos = jnp.where(keep, rank, capacity)
        disp = jnp.zeros((E, capacity + 1, D), x.dtype).at[se, pos].set(xf[st])
        disp = disp[:, :capacity]
        g = jnp.einsum('ecd,edf->ecf', disp, wg)
        u = jnp.einsum('ecd,edf->ecf', disp, wu)
        eo = jnp.einsum('ecf,efd->ecd', jax.nn.silu(g) * u, wd)
        gathered = eo[se, jnp.minimum(pos, capacity - 1)]
        contrib = gathered * (sw * keep.astype(x.dtype))[:, None]
        out = jnp.zeros_like(xf).at[st].add(contrib)
        return out.reshape(B, L, D)
    x = L0_attn_x
    x = _layernorm(x + _L0_attn_ref(x, L0_attn_w_qkv, L0_attn_b_qkv, L0_attn_w_out, L0_attn_b_out), axis=-1)
    x = _layernorm(x + _L0_ffn_ref(x, L0_ffn_Wqkv, L0_ffn_q_scale, L0_ffn_k_scale, L0_ffn_Wo, L0_ffn_ln_g, L0_ffn_ln_b, L0_ffn_W1, L0_ffn_b1, L0_ffn_W2, L0_ffn_b2), axis=-1)
    x = _layernorm(x + _L1_attn_ref(x, L1_attn_bind_key, L1_attn_unbind_key, L1_attn_gate, L1_attn_decay), axis=-1)
    x = _layernorm(x + _L1_ffn_ref(x, L1_ffn_router_w, L1_ffn_wg, L1_ffn_wu, L1_ffn_wd), axis=-1)
    return x

_drawn_inputs = setup_inputs


def setup_inputs(seed=0):
    import zlib

    import numpy as np

    out = dict(_drawn_inputs(seed))
    spreads = {'L0_attn_b_qkv': (0.0, 0.1),
     'L0_attn_b_out': (0.0, 0.1),
     'L0_ffn_q_scale': (1.0, 0.538),
     'L0_ffn_k_scale': (1.0, 0.594),
     'L0_ffn_ln_g': (1.0, 0.6),
     'L0_ffn_ln_b': (0.0, 0.64),
     'L0_ffn_b1': (0.0, 0.1),
     'L0_ffn_b2': (0.0, 0.1)}
    factors = {}
    for name, (base, spread) in spreads.items():
        noise = np.random.default_rng([zlib.crc32(name.encode()), seed]).standard_normal(out[name].shape)
        drawn = base * np.exp(spread * noise) if base else spread * noise
        out[name] = jnp.asarray(drawn.astype(out[name].dtype))
    for name, factor in factors.items():
        out[name] = (out[name] * factor).astype(out[name].dtype)
    return out
```

```python
import concourse.bass as bass
from concourse import mybir
from contextlib import ExitStack
import numpy as np

F32, BF16, I32 = mybir.dt.float32, mybir.dt.bfloat16, mybir.dt.int32
ALU, AF, AX = mybir.AluOpType, mybir.ActivationFunctionType, mybir.AxisListType
P = 128
B, SEQ, D = 2, 1024, 128
TB = SEQ // P
TILES = B * TB
DEPTH, HEADS, DH, WINDOW = 6, 16, 64, 32
INNER = HEADS * DH
FF = int(D * 4 * 2 / 3)
QK_SCALE = 8.0
EPS = 1e-5
MASKED = -float(2 ** 120)
NEWTON = 10


AH, AD = 16, 8
PARTS = 3
GH = 4
GROUPS = B * AH // GH
STACK = PARTS * PARTS * AD


def rope_tables():
    inv = np.power(np.float32(10000.0), -np.arange(0, AD, 2, dtype=np.float32) / np.float32(AD))
    ang = np.arange(SEQ, dtype=np.float32)[:, None] * inv[None, :]
    cos, sin = np.cos(ang), np.sin(ang)
    both = np.stack([np.repeat(cos, 2, axis=1), np.stack([-sin, sin], axis=2).reshape(SEQ, AD)], 0)
    return np.ascontiguousarray(np.tile(both.transpose(2, 0, 1), (AH, 1, 1)).astype(np.float32))


def layernorm_all(nc, src, dst, scratch, label="ln"):
    ctx = ExitStack()
    with ctx:
        def sb(name, shape):
            return ctx.enter_context(nc.sbuf_tensor(name, shape, F32))
        mean, var, rstd, half = (sb(f"{label}_{n}", [P, TILES]) for n in ("mean", "var", "rstd", "half"))
        step = ctx.enter_context(nc.semaphore("ln_step"))
        squared = ctx.enter_context(nc.semaphore("ln_squared"))
        rooted = ctx.enter_context(nc.semaphore("ln_rooted"))
        block = ctx.enter_context(nc.Block())

        def wide(t):
            return t[:, :].unsqueeze(2).broadcast_to([P, TILES, D])

        @block.vector
        def _(dve):
            dve.memset(half[:, :], -0.5).then_inc(step, 1)
            dve.tensor_reduce(mean[:, :], src[:, :, :], AX.X, ALU.add).then_inc(step, 1)
            dve.wait_ge(step, 2)
            dve.tensor_scalar(mean[:, :], mean[:, :], 1.0 / D, None, ALU.mult).then_inc(step, 1)
            dve.wait_ge(step, 3)
            dve.tensor_tensor(dst[:, :, :], src[:, :, :], wide(mean), ALU.subtract).then_inc(step, 1)
            dve.wait_ge(squared, 1)
            dve.tensor_reduce(var[:, :], scratch[:, :, :], AX.X, ALU.add).then_inc(step, 1)
            dve.wait_ge(step, 5)
            dve.tensor_scalar(var[:, :], var[:, :], 1.0 / D, EPS, ALU.mult, ALU.add).then_inc(step, 1)
            dve.wait_ge(rooted, 1)
            dve.tensor_tensor(dst[:, :, :], dst[:, :, :], wide(rstd), ALU.mult).then_inc(step, 1)
            dve.wait_ge(step, 7)

        @block.scalar
        def _(act):
            act.wait_ge(step, 4)
            act.activation(scratch[:, :, :], dst[:, :, :], AF.Square).then_inc(squared, 1)

        @block.gpsimd
        def _(pool):
            pool.wait_ge(step, 6)
            pool.tensor_tensor(rstd[:, :], var[:, :], half[:, :], ALU.pow).then_inc(rooted, 1)


def project_heads(nc, env, w, V):
    X, ident = env["X"], env["ident"]
    ctx = ExitStack()
    with ctx:
        def sb(name, shape, dt=F32):
            return ctx.enter_context(nc.sbuf_tensor(name, shape, dt))

        def sem(name):
            return ctx.enter_context(nc.semaphore(name))
        wr = sb("w_rows", [P, 5, D])
        wT = sb("w_turned", [P, 5, D])
        bias = sb("qk_bias", [P, 4])
        bv = sb("v_bias", [P, D])
        rope = sb("rope_tab", [P, 2, SEQ])
        xT = sb("xT_all", [P, B * SEQ])
        raw = sb("raw", [P, 4, 512])
        rot = sb("rot", [P, 2, 512])
        left = sb("left", [P, 2, 512])
        parts = [[sb(f"part{m}{j}", [P, 512], BF16) for j in range(PARTS)] for m in range(2)]
        bank = [ctx.enter_context(nc.psum_tensor(f"pP{r}", [P, 512], F32)) for r in range(4)]
        loaded, turned, kept, wready, wkept = sem("loaded"), sem("turned"), sem("kept"), sem("wready"), sem("wkept")
        qk_ready, biased, chain, split = sem("qk_ready"), sem("biased"), sem("chain"), sem("split")
        stored = [sem(f"stored{m}") for m in range(2)]
        v_ready, v_kept = sem("v_ready"), sem("v_kept")
        block = ctx.enter_context(nc.Block())
        bqkv = w["a_b_qkv"]
        LOADS = 3 + 4 + 2 + 4 + 1 + 1

        @block.sync
        def _(sp):
            for m, row in enumerate((0, 0, D, D, 2 * D)):
                src = w["a_w_qkv"][row:row + D, :]
                if m in (1, 3):
                    for e in range(2):
                        sp.dma_start(wr[e:P:2, m, :], src[1 - e:D:2, :]).then_inc(loaded, 16)
                else:
                    sp.dma_start(wr[:, m, :], src).then_inc(loaded, 16)
            for m, row in enumerate((0, 0, D, D)):
                src = bqkv[row:row + D].rearrange("(p a) -> p a", a=1)
                if m in (1, 3):
                    for e in range(2):
                        sp.dma_start(bias[e:P:2, m:m + 1], src[1 - e:D:2, :], allow_slow_non_contiguous=True).then_inc(loaded, 16)
                else:
                    sp.dma_start(bias[:, m:m + 1], src).then_inc(loaded, 16)
            sp.dma_start(bv[:, :], bqkv[2 * D:3 * D].rearrange("(a n) -> a n", a=1).broadcast_to([P, D])).then_inc(loaded, 16)
            sp.dma_start(rope[:, :, :], w["rope"]).then_inc(loaded, 16)
            for c in range(4):
                for m in range(2):
                    sp.wait_ge(split, 2 * c + m + 1)
                    for j in range(PARTS):
                        sp.dma_start(w["stacked"][m, j, :, 512 * c:512 * (c + 1)], parts[m][j][:, :]).then_inc(stored[m], 16)
            for m in range(2):
                sp.wait_ge(stored[m], 16 * 12)

        @block.tensor
        def _(pe):
            for n in range(4):
                for j in range(4):
                    mm = pe.transpose(bank[n][:, j * P:(j + 1) * P], X[:, 4 * n + j, :], ident[:, :])
                mm.then_inc(turned, 1)
            pe.wait_ge(loaded, 16 * LOADS)
            for m in range(5):
                pe.wait_ge(kept, m // 4 + 1 if m < 4 else 2)
                mm = pe.transpose(bank[m // 4][:, m % 4 * P:(m % 4 + 1) * P], wr[:, m, :], ident[:, :])
                if m >= 3:
                    mm.then_inc(wready, 1)
            pe.wait_ge(wkept, 2)
            pe.wait_ge(kept, 4)
            for c in range(4):
                for m in range(4):
                    if c:
                        pe.wait_ge(biased, 4 * (c - 1) + m + 1)
                    pe.matmul(bank[m][:, :], wT[:, m, :], xT[:, 512 * c:512 * (c + 1)], start=True, stop=True).then_inc(qk_ready, 1)
            for n in range(4):
                pe.wait_ge(biased, 12 + n + 1)
                for j in range(4):
                    t = 4 * n + j
                    mm = pe.matmul(bank[n][:, j * P:(j + 1) * P], xT[:, t * P:(t + 1) * P], wT[:, 4, :], start=True, stop=True)
                mm.then_inc(v_ready, 1)

        @block.scalar
        def _(act):
            for n in range(4):
                act.wait_ge(turned, n + 1)
                act.activation(xT[:, 512 * n:512 * (n + 1)], bank[n][:, :], AF.Copy).then_inc(kept, 1)
            act.wait_ge(wready, 1)
            act.activation(wT[:, 0:4, :], bank[0][:, :].rearrange("p (m n) -> p m n", m=4), AF.Copy).then_inc(wkept, 1)
            act.wait_ge(wready, 2)
            act.activation(wT[:, 4, :], bank[1][:, 0:P], AF.Copy).then_inc(wkept, 1)
            for c in range(4):
                for m in range(4):
                    act.wait_ge(qk_ready, 4 * c + m + 1)
                    if c:
                        act.wait_ge(chain, 2 * (6 * (c - 1)) + 6 * (m // 2) + 2)
                    act.activation(raw[:, m, :], bank[m][:, :], AF.Identity, bias=bias[:, m:m + 1]).then_inc(biased, 1)

        @block.vector
        def _(dve):
            dve.wait_ge(loaded, 16 * LOADS)
            n = 0
            for c in range(4):
                for m in range(2):
                    t = slice(512 * (c % 2), 512 * (c % 2) + 512)
                    r, lf = rot[:, m, :], left[:, m, :]
                    dve.wait_ge(biased, 4 * c + 2 * m + 2)
                    dve.tensor_tensor(r, raw[:, 2 * m, :], rope[:, 0, t], ALU.mult).then_inc(chain, 1)
                    dve.tensor_tensor(lf, raw[:, 2 * m + 1, :], rope[:, 1, t], ALU.mult).then_inc(chain, 1)
                    dve.wait_ge(chain, n + 2)
                    dve.tensor_tensor(r, r, lf, ALU.add).then_inc(chain, 1)
                    dve.wait_ge(chain, n + 3)
                    if c:
                        dve.wait_ge(stored[m], 48 * c)
                    dve.tensor_copy(parts[m][0][:, :], r).then_inc(chain, 1)
                    dve.wait_ge(chain, n + 4)
                    dve.tensor_tensor(lf, r, parts[m][0][:, :], ALU.subtract).then_inc(chain, 1)
                    dve.wait_ge(chain, n + 5)
                    dve.tensor_copy(parts[m][1][:, :], lf).then_inc(chain, 1)
                    dve.wait_ge(chain, n + 6)
                    dve.tensor_tensor(parts[m][2][:, :], lf, parts[m][1][:, :], ALU.subtract).then_inc(split, 1)
                    dve.wait_ge(split, 2 * c + m + 1)
                    n += 6
            for n in range(4):
                dve.wait_ge(v_ready, n + 1)
                dve.tensor_tensor(V[:, 4 * n:4 * n + 4, :], bank[n][:, :].rearrange("p (t n) -> p t n", t=4),
                                  bv[:, :].unsqueeze(1).broadcast_to([P, 4, D]), ALU.add).then_inc(v_kept, 1)
            dve.wait_ge(v_kept, 4)


def causal_attention(nc, env, w, V, O):
    identb, ident = env["identb"], env["ident"]
    CH = [(kt, q0, min(SEQ, (q0 // 512 + 1) * 512)) for kt in range(TB) for q0 in ([kt * P] if kt >= 4 else [kt * P, 512])]
    NT = len(CH) * GH
    NS = GH * TB
    NU = NS + 2
    LAG, RING = 2, 4

    ctx = ExitStack()
    with ctx:
        def sb(name, shape, dt=F32):
            return ctx.enter_context(nc.sbuf_tensor(name, shape, dt))

        def sem(name):
            return ctx.enter_context(nc.semaphore(name))
        QS = [sb(f"q_stack{r}", [P, GH, SEQ], BF16) for r in range(2)]
        KS = [sb(f"k_stack{r}", [P, GH, SEQ], BF16) for r in range(2)]
        flat = sb("zeros_ones", [3, 2, GH * SEQ], BF16)
        cm = sb("causal_by_query", [P, 2, P], BF16)
        NM = sb("minus_max", [P, NS])
        NL = sb("max_left", [P, NS])
        NP = sb("max_parts", [P, PARTS * NS], BF16)
        MT = sb("max_rows", [PARTS * NS, P], BF16)
        PTr = [sb(f"probs_by_key{r}", [P, 512]) for r in range(RING)]
        Vs = [sb(f"v_group{r}", [P, TB, GH, 32]) for r in range(2)]
        OS = sb("out_rows", [P, SEQ])
        den = sb("denominator", [P, 2, TB * GH])
        S = [ctx.enter_context(nc.psum_tensor(f"pS{r}", [P, SEQ], F32)) for r in range(2)]
        ST = [ctx.enter_context(nc.psum_tensor(f"pT{r}", [P, 512], F32)) for r in range(2)]
        OT = [ctx.enter_context(nc.psum_tensor(f"pO{r}", [P, 512], F32)) for r in range(2)]
        cleared = sem("cleared")
        cleared_p = sem("cleared_p")
        ones_in = sem("ones_in")
        stacks = [sem(f"stacks{r}") for r in range(2)]
        s_ready = sem("s_ready")
        s_free = sem("s_free")
        parts_done = sem("parts_done")
        rows_out = sem("rows_out")
        rows_in = sem("rows_in")
        v_copied = sem("v_copied")
        st_ready = sem("st_ready")
        exp_done = sem("exp_done")
        pv_done = sem("pv_done")
        o_kept = sem("o_kept")
        den_done = sem("den_done")
        block = ctx.enter_context(nc.Block())

        def ge(eng, sm, value):
            if isinstance(value, int) and value < 1:
                return
            eng.wait_ge(sm, value)

        def run(body):
            def program(eng):
                body(eng, 0, 0)
                body(eng, 1, 1)
                with eng.Fori(1, GROUPS // 2) as j:
                    body(eng, j * 2, 0)
                    body(eng, j * 2 + 1, 1)
                body(eng, GROUPS, 0)
            return program

        def has_s(it):
            return not isinstance(it, int) or it < GROUPS

        def has_t(it):
            return not isinstance(it, int) or it > 0

        def load_stacks(sp, g, par):
            r0 = (g % 4) * (GH * AD)
            c0 = (g // 4) * SEQ

            def src(m, j):
                if isinstance(g, int):
                    a = w["stacked"][m, j, r0:r0 + GH * AD, c0:c0 + SEQ]
                else:
                    a = w["stacked"][m, j, bass.ds(r0, GH * AD), bass.ds(c0, SEQ)]
                return a.rearrange("(h d) n -> d h n", d=AD)
            for j in range(PARTS):
                for k in range(PARTS):
                    at = (j * PARTS + k) * AD
                    sp.dma_start(QS[par][at:at + AD, :, :], src(0, j)).then_inc(stacks[par], 16)
                    sp.dma_start(KS[par][at:at + AD, :, :], src(1, k)).then_inc(stacks[par], 16)
            sp.dma_start(QS[par][STACK:STACK + 3, :, :], flat[:, 0, :].rearrange("p (h n) -> p h n", h=GH)).then_inc(stacks[par], 16)
        NLD = 2 * PARTS * PARTS + 1

        @block.sync
        def _(sp):
            sp.dma_start(cm[:, :, :], w["causal"]).then_inc(ones_in, 16)
            sp.wait_ge(cleared, 2)
            sp.wait_ge(cleared_p, 6)
            for r in range(2):
                sp.dma_start(KS[r][STACK:STACK + 3, :, :], flat[:, 1, :].rearrange("p (h n) -> p h n", h=GH)).then_inc(ones_in, 16)
            load_stacks(sp, 0, 0)

            def body(sp, it, par):
                if has_s(it):
                    sp.wait_ge(s_free, NU * it + NS + 1)
                    sp.dma_start(w["maxima"].rearrange("(r n) -> r n", n=P), MT[:, :]).then_inc(rows_out, 16)
                    sp.wait_ge(rows_out, 16 * it + 16)
                    sp.dma_start(QS[par][STACK:STACK + 3, :, :], w["maxima"].rearrange("(p h n) -> p h n", p=3, h=GH))\
                        .then_inc(rows_in, 16)
                if isinstance(it, int) and it + 1 >= GROUPS:
                    return
                if has_t(it):
                    sp.wait_ge(st_ready, NT * it)
                load_stacks(sp, it + 1, 1 - par)

            body(sp, 0, 0)
            body(sp, 1, 1)
            with sp.Fori(1, GROUPS // 2 - 1) as j:
                body(sp, j * 2, 0)
                body(sp, j * 2 + 1, 1)
            body(sp, GROUPS - 2, 0)
            body(sp, GROUPS - 1, 1)

        @block.tensor
        def _(pe):
            pe.wait_ge(ones_in, 48)
            pe.wait_ge(cleared_p, 6)

            def body(pe, it, par):
                g, tp = it - 1, 1 - par

                def row_block(u):
                    h, qt = divmod(u, TB)
                    if u == 0:
                        pe.wait_ge(stacks[par], (it // 2) * (16 * NLD) + 16 * NLD)
                    ge(pe, s_free, NU * it + u - 1)
                    n = (qt + 1) * P
                    for c in range(0, n, 512):
                        mm = pe.matmul(S[u % 2][:, c:min(n, c + 512)], QS[par][:, h, qt * P:n],
                                       KS[par][:, h, c:min(n, c + 512)], start=True, stop=True, skip_group_check=True)
                    mm = pe.matmul(S[u % 2][:, n - P:n], identb[:, :], cm[:, 0, :], start=False, stop=True, skip_group_check=True)
                    mm.then_inc(s_ready, 1)

                def chunk(n):
                    (kt, q0, q1), h = CH[n // GH], n % GH
                    if n == 0:
                        pe.wait_ge(rows_in, 16 * g + 16)
                    ge(pe, exp_done, NT * g + n - 1)
                    diag = q0 == kt * P
                    mm = pe.matmul(ST[n % 2][:, 0:q1 - q0], KS[tp][:, h, kt * P:(kt + 1) * P], QS[tp][:, h, q0:q1],
                                   start=True, stop=True, skip_group_check=True)
                    if diag:
                        mm = pe.matmul(ST[n % 2][:, 0:P], identb[:, :], cm[:, 1, :], start=False, stop=True, skip_group_check=True)
                    mm.then_inc(st_ready, 1)

                def values(n):
                    (kt, q0, q1), h = CH[n // GH], n % GH
                    if n == 0:
                        pe.wait_ge(v_copied, g + 1)
                        ge(pe, o_kept, 2 * g)
                    pe.wait_ge(exp_done, NT * g + n + 1)
                    qc = q0 // 512
                    last = kt == (3 if qc == 0 else TB - 1)
                    pe.matmul(OT[qc][32 * h:32 * h + 32, q0 - 512 * qc:q1 - 512 * qc], Vs[tp][:, kt, h, :],
                              PTr[n % RING][:, 0:q1 - q0], start=(kt == 0), stop=last, skip_group_check=True)\
                        .then_inc(pv_done, 1)

                done = 0
                for u in range(NS):
                    if has_s(it):
                        row_block(u)
                    if has_t(it):
                        for n in range(done, (u + 1) * NT // NS):
                            chunk(n)
                            if n >= LAG:
                                values(n - LAG)
                        done = (u + 1) * NT // NS
                if has_t(it):
                    for n in range(NT - LAG, NT):
                        values(n)
                at = NU * it
                if has_s(it):
                    pe.wait_ge(parts_done, 4 * it + 4)
                    pe.wait_ge(s_free, at + NS - 1)
                    pe.transpose(S[0][0:PARTS * NS, 0:P // 2].bitcast(BF16), NP[:, :], identb[:, :]).then_inc(s_ready, 1)
                    at = at + NS + 1
                if has_t(it):
                    pe.wait_ge(o_kept, 2 * g + 2)
                pe.wait_ge(s_free, at - 1 if has_s(it) else at)
                for t in range(TB):
                    mm = pe.transpose(S[1][:, t * P:(t + 1) * P], OS[:, t * P:(t + 1) * P], ident[:, :])
                mm.then_inc(s_ready, 1)
            run(body)(pe)

        @block.scalar
        def _(act):
            act.wait_ge(cleared, 2)
            def body(act, it, par):
                g = it - 1
                if not has_t(it):
                    return
                for n in range(NT):
                    kt, q0, q1 = CH[n // GH]
                    ge(act, pv_done, NT * g + n - RING + 1)
                    act.wait_ge(st_ready, NT * g + n + 1)
                    act.activation(PTr[n % RING][:, 0:q1 - q0], ST[n % 2][:, 0:q1 - q0], AF.Exp,
                                   scale=float(AD) ** -0.5).then_inc(exp_done, 1)
                act.wait_ge(s_ready, NU * it)
                for qc in range(2):
                    act.wait_ge(pv_done, NT * g + NT)
                    act.activation(OS[:, 512 * qc:512 * qc + 512], OT[qc][:, :], AF.Copy).then_inc(o_kept, 1)
            run(body)(act)

        @block.vector
        def _(dve):
            dve.memset(OS[:, :], 0.0).then_inc(cleared, 1)
            dve.memset(flat[:, 0, :], 0.0)
            dve.memset(flat[:, 1, :], 1.0).then_inc(cleared, 1)

            def body(dve, it, par):
                g = it - 1 if has_t(it) else 0
                at = NU * it
                if has_s(it):
                    for u in range(NS):
                        dve.wait_ge(s_ready, at + u + 1)
                        if u == 0:
                            ge(dve, parts_done, 4 * it)
                        dve.tensor_reduce(NM[:, u:u + 1], S[u % 2][:, 0:(u % TB + 1) * P], AX.X, ALU.max, negate=True)\
                            .then_inc(s_free, 1)
                    n = 4 * it
                    ge(dve, s_ready, at - 1)
                    dve.wait_ge(s_free, at + NS)
                    dve.tensor_copy(NP[:, 0:NS], NM[:, :]).then_inc(parts_done, 1)
                    dve.wait_ge(parts_done, n + 1)
                    dve.tensor_tensor(NL[:, :], NM[:, :], NP[:, 0:NS], ALU.subtract).then_inc(parts_done, 1)
                    dve.wait_ge(parts_done, n + 2)
                    dve.tensor_copy(NP[:, NS:2 * NS], NL[:, :]).then_inc(parts_done, 1)
                    dve.wait_ge(parts_done, n + 3)
                    dve.tensor_tensor(NP[:, 2 * NS:3 * NS], NL[:, :], NP[:, NS:2 * NS], ALU.subtract).then_inc(parts_done, 1)
                    dve.wait_ge(s_ready, at + NS + 1)
                    ge(dve, rows_out, 16 * it)
                    dve.tensor_copy(MT[:, :], S[0][0:PARTS * NS, 0:P // 2].bitcast(BF16)).then_inc(s_free, 1)
                    at = at + NS + 1
                dve.wait_ge(s_ready, at + 1)
                o4 = S[1][:, :].rearrange("p (t h d) -> p t h d", t=TB, h=GH)
                ge(dve, s_free, NU * it)
                dn = [den[:, k, :].rearrange("p (t h) -> p t h", t=TB) for k in range(2)]
                dve.tensor_scalar(dn[0].unsqueeze(3), o4[:, :, :, AD:AD + 1], 1e-8, None, ALU.add).then_inc(den_done, 1)
                dve.wait_ge(den_done, 2 * it + 1)
                dve.reciprocal(dn[1], dn[0]).then_inc(den_done, 1)
                dve.wait_ge(den_done, 2 * it + 2)
                r0, c0 = (g // 4) * TB, (g % 4) * (GH * AD)
                if isinstance(g, int):
                    out = O[:, r0:r0 + TB, c0:c0 + GH * AD]
                else:
                    out = O[:, bass.ds(r0, TB), bass.ds(c0, GH * AD)]
                dve.tensor_tensor(out.rearrange("p t (h d) -> p t h d", h=GH), o4[:, :, :, 0:AD],
                                  dn[1].unsqueeze(3).broadcast_to([P, TB, GH, AD]), ALU.mult).then_inc(s_free, 1)
                if isinstance(it, int) and it == 0:
                    dve.wait_ge(s_free, NU)
            run(body)(dve)

        @block.gpsimd
        def _(pool):
            for r in range(2):
                pool.memset(Vs[r][:, :, :, :], 0.0)
            for r in range(2):
                pool.memset(QS[r][:, :, :], 0.0).then_inc(cleared_p, 1)
                pool.memset(KS[r][:, :, :], 0.0).then_inc(cleared_p, 1)
            pool.wait_ge(cleared_p, 4)
            for r in range(2):
                pool.memset(Vs[r][:, :, :, AD:AD + 1], 1.0).then_inc(cleared_p, 1)
            pool.wait_ge(cleared_p, 6)

            def body(pool, it, par):
                g, tp = it - 1, 1 - par
                if not has_t(it):
                    return
                ge(pool, pv_done, NT * (g - 1))
                r0, c0 = (g // 4) * TB, (g % 4) * (GH * AD)
                if isinstance(g, int):
                    src = V[:, r0:r0 + TB, c0:c0 + GH * AD]
                else:
                    src = V[:, bass.ds(r0, TB), bass.ds(c0, GH * AD)]
                pool.tensor_copy(Vs[tp][:, :, :, 0:AD], src.rearrange("p t (h d) -> p t h d", h=GH)).then_inc(v_copied, 1)
            run(body)(pool)


def project_out(nc, env, w, O, Z):
    X, ident = env["X"], env["ident"]
    ctx = ExitStack()
    with ctx:
        def sb(name, shape, dt=F32):
            return ctx.enter_context(nc.sbuf_tensor(name, shape, dt))

        def sem(name):
            return ctx.enter_context(nc.semaphore(name))
        wo = sb("wo_rows", [P, D])
        woT = sb("wo_turned", [P, D])
        bo = sb("b_out", [P, D])
        OT = sb("o_turned", [P, TILES, P])
        bank = [ctx.enter_context(nc.psum_tensor(f"pR{r}", [P, 512], F32)) for r in range(8)]
        loaded, w_ready, w_kept, t_ready, t_kept, y_ready, y_kept, xb = (sem(n) for n in (
            "loaded", "w_ready", "w_kept", "t_ready", "t_kept", "y_ready", "y_kept", "xb"))
        block = ctx.enter_context(nc.Block())

        @block.sync
        def _(sp):
            sp.dma_start(wo[:, :], w["a_w_out"]).then_inc(loaded, 16)
            sp.dma_start(bo[:, :], w["a_b_out"].rearrange("(a n) -> a n", a=1).broadcast_to([P, D])).then_inc(loaded, 16)

        @block.tensor
        def _(pe):
            pe.wait_ge(loaded, 32)
            pe.transpose(bank[4][:, 0:P], wo[:, :], ident[:, :]).then_inc(w_ready, 1)
            for n in range(4):
                for j in range(4):
                    mm = pe.transpose(bank[n][:, j * P:(j + 1) * P], O[:, 4 * n + j, :], ident[:, :])
                mm.then_inc(t_ready, 1)
            pe.wait_ge(w_kept, 1)
            for n in range(4):
                pe.wait_ge(t_kept, n + 1)
                for j in range(4):
                    mm = pe.matmul(bank[4 + n][:, j * P:(j + 1) * P], OT[:, 4 * n + j, :], woT[:, :], start=True, stop=True)
                mm.then_inc(y_ready, 1)

        @block.scalar
        def _(act):
            act.wait_ge(w_ready, 1)
            act.activation(woT[:, :], bank[4][:, 0:P], AF.Copy).then_inc(w_kept, 1)
            for n in range(4):
                act.wait_ge(t_ready, n + 1)
                act.activation(OT[:, 4 * n:4 * n + 4, :], bank[n][:, :].rearrange("p (t n) -> p t n", t=4), AF.Copy).then_inc(t_kept, 1)

        @block.vector
        def _(dve):
            dve.wait_ge(loaded, 32)
            dve.tensor_tensor(X[:, :, :], X[:, :, :], bo[:, :].unsqueeze(1).broadcast_to([P, TILES, D]), ALU.add).then_inc(xb, 1)
            dve.wait_ge(xb, 1)
            for n in range(4):
                dve.wait_ge(y_ready, n + 1)
                dve.tensor_tensor(Z[:, 4 * n:4 * n + 4, :], X[:, 4 * n:4 * n + 4, :],
                                  bank[4 + n][:, :].rearrange("p (t n) -> p t n", t=4), ALU.add).then_inc(y_kept, 1)
            dve.wait_ge(y_kept, 4)


def causal_masks():
    m = np.where(np.arange(P)[None, :] > np.arange(P)[:, None], MASKED, 0.0).astype(np.float32)
    return np.stack([m, m.T], axis=1)


def xpos_tables():
    half = np.arange(0, DH, 2, dtype=np.float32)
    inv_freq = np.float32(1.0) / np.power(np.float32(10000.0), half / np.float32(DH))
    token = np.arange(SEQ, dtype=np.float32)
    freqs = token[:, None] * inv_freq[None, :]
    base = (half + np.float32(0.4 * DH)) / np.float32(1.4 * DH)
    power = (token - SEQ // 2) / np.float32(WINDOW // 2)
    scale = np.power(base[None, :], power[:, None])
    cos, sin, inv = np.cos(freqs), np.sin(freqs), np.float32(1.0) / scale
    rows = [cos * scale, cos * scale, -sin * scale, sin * scale, cos * inv, cos * inv, -sin * inv, sin * inv]
    table = np.concatenate(rows, axis=1).astype(np.float32)
    return np.ascontiguousarray(table.reshape(TB, P, 4 * DH).transpose(1, 0, 2))


def window_mask():
    query = np.arange(WINDOW)[:, None]
    key = np.arange(2 * WINDOW)[None, :]
    hidden = (key > query + WINDOW) | (key < query)
    mask = np.zeros((2, 2, WINDOW, TB, 2, 2 * WINDOW), np.float32)
    mask[:] = np.where(hidden, MASKED, 0.0)[:, None, None, :]
    mask[0, :, :, 0, 0, :WINDOW] = MASKED
    return mask.reshape(P, TB, 4 * WINDOW)


def window_layers(nc, env, w):
    STEPS = DEPTH * TILES
    X, ident, identb = env["X"], env["ident"], env["identb"]
    QKV_AT, WO_AT = 0, 3 * INNER
    W1_AT = WO_AT + 8 * D
    W2_AT = W1_AT + 2 * FF
    B1_AT = W2_AT + 3 * D
    B2_AT = B1_AT + 2 * FF
    SC_AT = B2_AT + D
    LN_AT = SC_AT + 4 * DH
    SLOT = LN_AT + 2
    R = FF - 2 * P

    ctx = ExitStack()
    with ctx:
        def sb(name, shape, dt=F32):
            return ctx.enter_context(nc.sbuf_tensor(name, shape, dt))

        def sem(name):
            return ctx.enter_context(nc.semaphore(name))

        def banks(name):
            return [ctx.enter_context(nc.psum_tensor(f"{name}{r}", [P, 512], F32)) for r in range(2)]

        W = sb("layer_weights", [P, 2 * SLOT])
        tab = sb("xpos_tab", [P, TB, 4 * DH])
        tabl = sb("layer_tab", [P, 4, 2, 32])
        mask = sb("window_mask", [P, TB, 4 * WINDOW], BF16)
        X0f = sb("x_feature_major", [P, B * (SEQ + 1)])
        X1f = sb("x1_feature_major", [P, B * (SEQ + 1)])
        xsT = [sb(f"xsT{r}", [P, P]) for r in range(2)]
        sq = [sb(f"sq{r}", [P, 512]) for r in range(2)]
        t1 = [sb(f"rot_cos{r}", [P, 512]) for r in range(2)]
        t2 = [sb(f"rot_sin{r}", [P, 512]) for r in range(2)]
        ss = sb("sumsq", [P, 32])
        rn = [sb(f"rnorm{r}", [P, 32]) for r in range(2)]
        nw = sb("newton", [P, 4, 32])
        QK = [sb(f"qk{r}", [P, 4, 512]) for r in range(2)]
        qT = [sb(f"qT{r}", [P, 8, 4, 2, 32]) for r in range(2)]
        kT = [sb(f"kT{r}", [P, 8, 160]) for r in range(2)]
        V = [sb(f"v{r}", [P, INNER]) for r in range(2)]
        Vt = [sb(f"v_tail{r}", [P, 16, DH]) for r in range(2)]
        mx = sb("row_max", [P, 16])
        E = [sb(f"probs{r}", [P, 16, 64]) for r in range(2)]
        rs = sb("row_sum", [P, 2, 16])
        PA = [sb(f"probs_placed{r}", [P, 16, P]) for r in range(2)]
        PB = [sb(f"probs_before{r}", [32, 16, 32]) for r in range(2)]
        PT = sb("probsT", [P, 16, P])
        PTp = sb("probsT_before", [P, 4, 32])
        oT = sb("attn_outT", [P, 8, P])
        xc = [sb(f"x1_tile{r}", [P, D]) for r in range(2)]
        xs1 = sb("xs1T", [P, P])
        st = sb("ln_stats", [P, 6])
        mv = sb("ln_mean_var", [P, 2])
        ve = sb("ln_var_eps", [P, 1])
        rstd = sb("ln_rstd", [P, 1])
        mhalf = sb("minus_half", [P, 1])
        xn = sb("xn", [P, D])
        xnT = sb("xnT", [P, P])
        ha = sb("ff_a", [P, FF])
        hg = sb("ff_gate", [P, FF])
        hm = sb("ff_mid", [P, 3 * P])
        hT = sb("ff_midT", [P, 3, P])
        xb2 = sb("x1_b2", [P, D])
        x2 = sb("x2_tile", [P, D])

        A, C, Db, E4 = banks("pA"), banks("pC"), banks("pD"), banks("pE")

        w_loaded = sem("w_loaded")
        const_loaded = sem("const_loaded")
        zeroed = sem("zeroed")
        zeroed_p = sem("zeroed_p")
        x_turned = sem("x_turned")
        xT_ready = sem("xT_ready")
        xs_ready = sem("xs_ready")
        a_ready = sem("a_ready")
        sq_done = sem("sq_done")
        ss_done = sem("ss_done")
        rot_done = sem("rot_done")
        tab_done = sem("tab_done")
        nw_done = sem("nw_done")
        rn_done = sem("rn_done")
        added = sem("added")
        scaled = sem("scaled")
        c_ready = sem("c_ready")
        free_c = [sem(f"free_c{r}") for r in range(2)]
        kprev = sem("kprev")
        mx_done = sem("mx_done")
        exp_done = sem("exp_done")
        sum_done = sem("sum_done")
        rsum_done = sem("rsum_done")
        pn_done = sem("pn_done")
        placed = sem("placed")
        vt_done = sem("vt_done")
        d_ready = sem("d_ready")
        free_d = [sem(f"free_d{r}") for r in range(2)]
        e_ready = sem("e_ready")
        free_e = [sem(f"free_e{r}") for r in range(2)]
        xs1_done = sem("xs1_done")
        ln_chain = sem("ln_chain")
        rstd_done = sem("rstd_done")
        gelu_done = sem("gelu_done")
        hm_done = sem("hm_done")
        xb2_done = sem("xb2_done")
        x_kept = sem("x_kept")

        block = ctx.enter_context(nc.Block())

        def slot(s, at, n):
            if isinstance(s, int):
                o = (s // TILES) % 2 * SLOT + at
                return W[:, o:o + n]
            return W[:, bass.ds((s // TILES) % 2 * SLOT + at, n)]

        def cols(t, s, half=None):
            o = (s // TB) % 2 * (SEQ + 1) + s % TB * P + (half or 0)
            rows = slice(None) if half is None else slice(64 * half, 64 * half + 64)
            return t[rows, o:o + P] if isinstance(s, int) else t[rows, bass.ds(o, P)]

        def tile_of(t, s, n):
            return t[:, s % n, :] if isinstance(s, int) else t[:, bass.ds(s % n, 1), :]

        def ge(eng, sm, value):
            if isinstance(value, int) and value < 1:
                return
            eng.wait_ge(sm, value)

        def run(body):
            def it(eng, i, par):
                live = [not isinstance(i, int) or 0 <= i - k < STEPS for k in range(4)]
                body(eng, i, par, live)

            def program(eng):
                for i in range(4):
                    it(eng, i, i % 2)
                with eng.Fori(2, STEPS // 2) as j:
                    it(eng, j * 2, 0)
                    it(eng, j * 2 + 1, 1)
                for i in range(STEPS, STEPS + 3):
                    it(eng, i, i % 2)
            return program

        def load_layer(sp, l):
            o = l % 2 * SLOT
            for c in range(4):
                sp.dma_start(W[:, o + c * 768:o + (c + 1) * 768], w["Wqkv"][l, :, c * 768:(c + 1) * 768]).then_inc(w_loaded, 16)
            sp.dma_start(W[:, o + WO_AT:o + W1_AT].rearrange("p (g n) -> p g n", n=D),
                         w["Wo"][l].rearrange("(g p) n -> p g n", p=P)).then_inc(w_loaded, 16)
            sp.dma_start(W[:, o + W1_AT:o + W2_AT], w["W1"][l]).then_inc(w_loaded, 16)
            for j, (src, h) in enumerate((("q_scale", 0), ("q_scale", 1), ("k_scale", 0), ("k_scale", 1))):
                at = o + SC_AT + j * DH
                if h == 0:
                    sp.dma_start(W[:, at:at + DH], w[src][l:l + 1, :].broadcast_to([P, DH])).then_inc(w_loaded, 16)
                else:
                    sp.dma_start(W[:, at:at + 32], w[src][l:l + 1, 32:64].broadcast_to([P, 32])).then_inc(w_loaded, 16)
                    sp.dma_start(W[:, at + 32:at + 64], w[src][l:l + 1, 0:32].broadcast_to([P, 32])).then_inc(w_loaded, 16)
            sp.dma_start(W[:, o + W2_AT:o + W2_AT + 2 * D].rearrange("p (g n) -> p g n", n=D),
                         w["W2"][l, 0:2 * P, :].rearrange("(g p) n -> p g n", p=P)).then_inc(w_loaded, 16)
            sp.dma_start(W[0:R, o + W2_AT + 2 * D:o + W2_AT + 3 * D], w["W2"][l, 2 * P:FF, :]).then_inc(w_loaded, 16)
            sp.dma_start(W[:, o + B1_AT:o + B1_AT + 2 * FF], w["b1"][l:l + 1, :].broadcast_to([P, 2 * FF])).then_inc(w_loaded, 16)

        def load_layer_tail(sp, l):
            o = l % 2 * SLOT
            sp.dma_start(W[:, o + B2_AT:o + B2_AT + D], w["b2"][l:l + 1, :].broadcast_to([P, D])).then_inc(w_loaded, 16)
            sp.dma_start(W[:, o + LN_AT:o + LN_AT + 1], w["ln_g"][l, :].rearrange("(p a) -> p a", a=1)).then_inc(w_loaded, 16)
            sp.dma_start(W[:, o + LN_AT + 1:o + LN_AT + 2], w["ln_b"][l, :].rearrange("(p a) -> p a", a=1)).then_inc(w_loaded, 16)
        NW = 15 + 3

        @block.sync
        def _(sp):
            sp.dma_start(tab[:], w["xpos"]).then_inc(const_loaded, 16)
            sp.dma_start(mask[:], w["mask"]).then_inc(const_loaded, 16)
            sp.wait_ge(zeroed, 1)
            for l in range(2):
                load_layer(sp, l)
                load_layer_tail(sp, l)
                sp.wait_ge(w_loaded, 16 * NW * (l + 1))
            sp.wait_ge(zeroed_p, 1)

            def place(s, par):
                sp.wait_ge(pn_done, s + 1)
                for j in range(2):
                    for b in range(2):
                        for wp in range(2):
                            q = 32 * (2 * wp + j)
                            src = E[par][64 * j + 32 * b:64 * j + 32 * b + 32].rearrange("p (h w) k -> p h w k", w=2)
                            skip = 32 if q == 0 else 0
                            sp.dma_start(PA[par][q:q + 32].rearrange("p (h b) k -> p h b k", b=2)[:, :, b, q + skip - 32:q + 32],
                                         src[:, :, wp, skip:]).then_inc(placed, 16)
                            if q == 0:
                                sp.dma_start(PB[par][:, :, :].rearrange("p (h b) k -> p h b k", b=2)[:, :, b, :],
                                             src[:, :, wp, 0:32]).then_inc(placed, 16)
                if isinstance(s, int):
                    for r in range(2):
                        sp.wait_ge(free_c[r], 4 * s + 4)
                    ge(sp, d_ready, 8 * (s - 1) + 7)
                else:
                    sp.wait_ge(x_kept, s - 1)
                for j in range(4):
                    sp.dma_start(Vt[par][32 * j:32 * j + 32].rearrange("p (g j) d -> p g j d", j=4)[:, :, j, :],
                                 V[par][96:128].rearrange("p (g j d) -> p g j d", j=4, d=DH)[:, :, j, :])\
                        .then_inc(vt_done, 16)

            place(0, 0)
            place(1, 1)
            at = 1
            for l in range(2, DEPTH + 1):
                until = 8 * (l - 1) + 2 if l < DEPTH else STEPS // 2
                with sp.Fori(at, until) as j:
                    place(j * 2, 0)
                    place(j * 2 + 1, 1)
                at = until
                if l < DEPTH:
                    sp.wait_ge(xT_ready, TILES + TILES * (l - 1))
                    load_layer(sp, l)
                    load_layer_tail(sp, l)
                    sp.wait_ge(w_loaded, 16 * NW * (l + 1))

        def pe_body(pe, i, par, live):
            s1, s2, s3, s4 = i, i - 1, i - 2, i - 3
            op = 1 - par

            def T(u):
                if not live[1]:
                    return
                pe.wait_ge(scaled, 4 * s2 + u + 1)
                ge(pe, free_c[u % 2], 4 * s2 + u // 2)
                for j in range(4):
                    mm = pe.transpose(C[u % 2][:, j * P:(j + 1) * P], QK[op][:, u, j * P:(j + 1) * P], ident[:, :])
                mm.then_inc(c_ready, 1)

            def QKc(c):
                if not live[0]:
                    return
                if c == 0:
                    pe.wait_ge(xs_ready, s1 + 1)
                    pe.wait_ge(w_loaded, (s1 // TILES) * (16 * NW) + 16 * NW)
                ge(pe, rot_done, 4 * s1 + c - 1)
                pe.matmul(A[c % 2][:, :], xsT[par][:, :], slot(s1, QKV_AT + 512 * c, 512), start=True, stop=True)\
                    .then_inc(a_ready, 1)

            def S(u):
                if not live[1]:
                    return
                for r in range(2):
                    pe.wait_ge(free_c[r], 4 * s2 + 2)
                ge(pe, kprev, 2 * s2)
                pe.matmul(C[u][:, :], identb[:, :], tile_of(mask, s2, TB).broadcast_to([P, 4, P]) if not isinstance(s2, int)
                          else mask[:, s2 % TB, :].unsqueeze(1).broadcast_to([P, 4, P]), start=True, stop=True, skip_group_check=True)
                for hp in range(4):
                    for wi in range(4):
                        j, wp = wi % 2, wi // 2
                        mm = pe.matmul(C[u][64 * j:64 * j + 64, hp * P + 64 * wp:hp * P + 64 * wp + 64],
                                       qT[op][:, 4 * u + hp, wi, :, :], kT[op][:, 4 * u + hp, 32 * wi:32 * wi + 64],
                                       start=False, stop=True, skip_group_check=True)
                mm.then_inc(c_ready, 1)

            def Vc(v):
                if not live[1]:
                    return
                pe.wait_ge(free_c[v], 4 * s2 + 3)
                pe.matmul(C[v][:, :], xsT[op][:, :], slot(s2, QKV_AT + 2 * INNER + 512 * v, 512), start=True, stop=True)\
                    .then_inc(c_ready, 1)

            def PTb():
                if not live[2]:
                    return
                for g in range(4):
                    mm = pe.transpose(Db[0][:, 32 * g:32 * g + 32], PB[par][:, 4 * g:4 * g + 4, :], ident[0:32, 0:32])
                mm.then_inc(d_ready, 1)

            def PTo(k):
                if not live[2]:
                    return
                n = (1, 2, 4, 5)[k]
                if k == 0:
                    pe.wait_ge(placed, 160 * s3 + 160)
                    ge(pe, free_d[0], 4 * s3)
                ge(pe, free_d[n % 2], 4 * s3 + n // 2)
                for j in range(4):
                    mm = pe.transpose(Db[n % 2][:, j * P:(j + 1) * P], PA[par][:, 4 * k + j, :], ident[:, :])
                mm.then_inc(d_ready, 1)

            def O(u):
                if not live[2]:
                    return
                n = (3, 6)[u]
                pe.wait_ge(free_d[0], 4 * s3 + 2 + u)
                pe.wait_ge(free_d[1], 4 * s3 + 1 + 2 * u)
                ge(pe, vt_done, 64 * s3)
                for r in range(2):
                    pe.wait_ge(free_c[r], 4 * s3 + 4)
                for h in range(8 * u, 8 * u + 8):
                    o = Db[n % 2][64 * (h % 2):64 * (h % 2) + 64, h // 2 % 4 * P:(h // 2 % 4 + 1) * P]
                    pe.matmul(o, V[par][:, h * DH:(h + 1) * DH], PT[:, h, :], start=True, stop=False, skip_group_check=True)
                    mm = pe.matmul(o[:, 0:32], Vt[op][:, h, :], PTp[:, h // 4, :], start=False, stop=True, skip_group_check=True)
                mm.then_inc(d_ready, 1)

            def Y():
                if not live[2]:
                    return
                pe.wait_ge(free_d[0], 4 * s3 + 4)
                pe.wait_ge(free_d[1], 4 * s3 + 3)
                for g in range(8):
                    mm = pe.matmul(Db[1][:, 0:D], oT[:, g, :], slot(s3, WO_AT + g * D, D), start=(g == 0), stop=(g == 7))
                mm.then_inc(d_ready, 1)

            def X1T():
                if not live[3]:
                    return
                pe.wait_ge(free_d[1], 4 * s4 + 4)
                ge(pe, free_e[0], 4 * s4)
                pe.transpose(E4[0][:, 0:P], xc[op][:, :], ident[:, :]).then_inc(e_ready, 1)

            def L1():
                if not live[3]:
                    return
                pe.wait_ge(xs1_done, s4 + 1)
                pe.wait_ge(xT_ready, TILES + s4)
                pe.transpose(E4[1][:, 0:P], xs1[:, :], ident[:, :]).then_inc(e_ready, 1)

            def L2():
                if not live[3]:
                    return
                pe.wait_ge(free_e[1], 3 * s4 + 1)
                pe.wait_ge(free_e[0], 4 * s4 + 1)
                pe.transpose(E4[0][:, 0:P], xn[:, :], ident[:, :]).then_inc(e_ready, 1)

            def W1():
                if not live[3]:
                    return
                pe.wait_ge(free_e[0], 4 * s4 + 2)
                for r in (1, 0):
                    pe.matmul(E4[r][:, 0:FF], xnT[:, :], slot(s4, W1_AT + (1 - r) * FF, FF), start=True, stop=True)\
                        .then_inc(e_ready, 1)

            def HT():
                if not live[3]:
                    return
                pe.wait_ge(hm_done, s4 + 1)
                pe.wait_ge(free_e[1], 3 * s4 + 2)
                for g in range(3):
                    mm = pe.transpose(E4[1][:, g * P:(g + 1) * P], hm[:, g * P:(g + 1) * P], ident[:, :])
                mm.then_inc(e_ready, 1)

            def W2():
                if not live[3]:
                    return
                pe.wait_ge(free_e[1], 3 * s4 + 3)
                pe.wait_ge(free_e[0], 4 * s4 + 3)
                for g in range(3):
                    mm = pe.matmul(E4[0][:, 0:D], hT[:, g, :], slot(s4, W2_AT + g * D, D), start=(g == 0), stop=(g == 2))
                mm.then_inc(e_ready, 1)

            def X2T():
                if not live[3]:
                    return
                pe.wait_ge(free_e[0], 4 * s4 + 4)
                pe.transpose(E4[1][:, 0:P], x2[:, :], ident[:, :]).then_inc(e_ready, 1)

            T(0)
            QKc(0)
            T(1)
            X1T()
            QKc(1)
            T(2)
            T(3)
            L1()
            S(0)
            PTo(0)
            PTb()
            QKc(2)
            QKc(3)
            L2()
            PTo(1)
            S(1)
            O(0)
            Vc(0)
            Vc(1)
            W1()
            PTo(2)
            PTo(3)
            O(1)
            HT()
            Y()
            W2()
            X2T()

        @block.tensor
        def _(pe):
            for n, bank in enumerate((A[0], A[1], C[0], C[1])):
                for j in range(4):
                    mm = pe.transpose(bank[:, j * P:(j + 1) * P], X[:, 4 * n + j, :], ident[:, :])
                mm.then_inc(x_turned, 1)
            pe.wait_ge(xT_ready, TILES)
            pe.wait_ge(const_loaded, 32)
            pe.wait_ge(zeroed, 9)
            pe.wait_ge(zeroed_p, 3)
            run(pe_body)(pe)

        def act_body(act, i, par, live):
            s1, s2, s3, s4 = i, i - 1, i - 2, i - 3
            op = 1 - par

            def T(u):
                if not live[1]:
                    return
                act.wait_ge(c_ready, 8 * s2 + u + 1)
                if u < 2:
                    for b in range(2):
                        r = slice(64 * b, 64 * b + 64)
                        a = act.activation(qT[op][r, 4 * u:4 * u + 4, :, b, :],
                                           C[u % 2][r, :].rearrange("p (h w q) -> p h w q", h=4, w=4), AF.Copy)
                else:
                    keys = C[u % 2][:, :].rearrange("p (h q) -> p h q", h=4)
                    h = slice(4 * (u - 2), 4 * (u - 2) + 4)
                    ge(act, c_ready, 8 * (s2 - 1) + 6)
                    act.activation(kT[par][:, h, 0:32], keys[:, :, 96:128], AF.Copy).then_inc(kprev, 1)
                    a = act.activation(kT[op][:, h, 32:160], keys, AF.Copy)
                a.then_inc(free_c[u % 2], 1)

            def square(c):
                if not live[0]:
                    return
                act.wait_ge(a_ready, 4 * s1 + c + 1)
                ge(act, ss_done, 4 * s1 + c - 1)
                act.activation(sq[c % 2][:, :], A[c % 2][:, :], AF.Square).then_inc(sq_done, 1)

            def exp(u):
                if not live[1]:
                    return
                act.wait_ge(free_c[u], 4 * s2 + 3)
                act.activation(E[op][:, 8 * u:8 * u + 8, :], E[op][:, 8 * u:8 * u + 8, :], AF.Exp, scale=QK_SCALE)\
                    .then_inc(exp_done, 1)

            def Vc(v):
                if not live[1]:
                    return
                act.wait_ge(c_ready, 8 * s2 + 7 + v)
                ge(act, d_ready, 8 * (s2 - 2) + 7)
                ge(act, vt_done, 64 * (s2 - 1))
                act.activation(V[op][:, 512 * v:512 * v + 512], C[v][:, :], AF.Copy).then_inc(free_c[v], 1)

            def PTb():
                if not live[2]:
                    return
                act.wait_ge(d_ready, 8 * s3 + 2)
                act.activation(PTp[:, :, :], Db[0][:, 0:P].rearrange("p (g q) -> p g q", g=4), AF.Copy).then_inc(free_d[0], 1)

            def PTo(k):
                if not live[2]:
                    return
                n = (1, 2, 4, 5)[k]
                act.wait_ge(d_ready, 8 * s3 + (n + 1 if k else 1))
                act.activation(PT[:, 4 * k:4 * k + 4, :], Db[n % 2][:, :].rearrange("p (h q) -> p h q", h=4), AF.Copy)\
                    .then_inc(free_d[n % 2], 1)

            def O(u):
                if not live[2]:
                    return
                n = (3, 6)[u]
                act.wait_ge(d_ready, 8 * s3 + n + 1)
                act.activation(oT[:, 4 * u:4 * u + 4, :], Db[n % 2][:, :].rearrange("p (h q) -> p h q", h=4), AF.Copy)\
                    .then_inc(free_d[n % 2], 1)

            def X1T():
                if not live[3]:
                    return
                act.wait_ge(e_ready, 8 * s4 + 1)
                ge(act, xs1_done, s4)
                act.activation(cols(X1f, s4, 0), E4[0][0:64, 0:P], AF.Copy)
                act.activation(cols(X1f, s4, 1), E4[0][64:128, 0:P], AF.Copy).then_inc(free_e[0], 1)

            def L2():
                if not live[3]:
                    return
                act.wait_ge(e_ready, 8 * s4 + 3)
                act.activation(xnT[:, :], E4[0][:, 0:P], AF.Identity, scale=slot(s4, LN_AT, 1), bias=slot(s4, LN_AT + 1, 1))\
                    .then_inc(free_e[0], 1)

            def gelu():
                if not live[3]:
                    return
                act.wait_ge(free_e[0], 4 * s4 + 3)
                act.activation(hg[:, :], hg[:, :], AF.Gelu).then_inc(gelu_done, 1)

            def HT():
                if not live[3]:
                    return
                act.wait_ge(e_ready, 8 * s4 + 6)
                act.activation(hT[:, :, :], E4[1][:, 0:3 * P].rearrange("p (g q) -> p g q", g=3), AF.Copy).then_inc(free_e[1], 1)

            def X2T():
                if not live[3]:
                    return
                act.wait_ge(e_ready, 8 * s4 + 8)
                act.activation(cols(X0f, s4, 0), E4[1][0:64, 0:P], AF.Copy)
                act.activation(cols(X0f, s4, 1), E4[1][64:128, 0:P], AF.Copy).then_inc(xT_ready, 1)

            T(0)
            square(0)
            T(1)
            X1T()
            square(1)
            T(2)
            T(3)
            PTo(0)
            PTb()
            square(2)
            square(3)
            L2()
            PTo(1)
            exp(0)
            exp(1)
            Vc(0)
            O(0)
            Vc(1)
            PTo(2)
            PTo(3)
            gelu()
            O(1)
            HT()
            X2T()

        @block.scalar
        def _(act):
            for n, bank in enumerate((A[0], A[1], C[0], C[1])):
                act.wait_ge(x_turned, n + 1)
                for j in range(4):
                    for half in range(2):
                        a = act.activation(cols(X0f, 4 * n + j, half), bank[64 * half:64 * half + 64, j * P:(j + 1) * P], AF.Copy)
                    a.then_inc(xT_ready, 1)
            act.wait_ge(zeroed, 9)
            act.wait_ge(zeroed_p, 3)
            run(act_body)(act)

        def dve_body(dve, i, par, live):
            s1, s2, s3, s4 = i, i - 1, i - 2, i - 3
            op = 1 - par

            def table():
                if not live[0]:
                    return
                dve.wait_ge(w_loaded, (s1 // TILES) * (16 * NW) + 16 * NW)
                ge(dve, rot_done, 4 * s1)
                tb = tab[:, s1 % TB, :] if isinstance(s1, int) else tab[:, bass.ds(s1 % TB, 1), :]
                dve.tensor_tensor(tabl[:, :, :, :], tb, slot(s1, SC_AT, 4 * DH), ALU.mult).then_inc(tab_done, 1)

            def rotate(c, after_stats=False):
                if after_stats:
                    dve.wait_ge(ln_chain, 3 * s4 + 1)
                    ge(dve, free_e[1], 3 * s4)
                if not live[0]:
                    return
                a = A[c % 2][:, :].rearrange("p (h g d) -> p h g d", g=2, d=32)
                k = c // 2 * 2
                dve.wait_ge(sq_done, 4 * s1 + c + 1)
                if c == 0:
                    dve.wait_ge(tab_done, s1 + 1)
                ge(dve, added, 4 * s1 + c - 1)
                dve.tensor_tensor(t1[c % 2][:, :].rearrange("p (h g d) -> p h g d", g=2, d=32), a,
                                  tabl[:, k].unsqueeze(1).broadcast_to([P, 8, 2, 32]), ALU.mult)
                dve.tensor_tensor(t2[c % 2][:, :].rearrange("p (h g d) -> p h g d", g=2, d=32), a[:, :, ::-1, :],
                                  tabl[:, k + 1].unsqueeze(1).broadcast_to([P, 8, 2, 32]), ALU.mult).then_inc(rot_done, 1)
                if c == 0:
                    ge(dve, nw_done, NEWTON * s1)
                dve.tensor_reduce(ss[:, 8 * c:8 * c + 8], sq[c % 2][:, :].rearrange("p (h d) -> p h d", d=DH),
                                  AX.X, ALU.add).then_inc(ss_done, 1)

            def newton():
                if not live[0]:
                    return
                base = NEWTON * s1
                x, y, y2, z = (nw[:, k, :] for k in range(4))
                dve.wait_ge(ss_done, 4 * s1 + 4)
                dve.tensor_scalar(x, ss[:, :], 1e-24, None, ALU.max).then_inc(nw_done, 1)
                dve.wait_ge(nw_done, base + 1)
                dve.tensor_scalar(y.bitcast(I32), x.bitcast(I32), -0.5, float(0x5F3759DF), ALU.mult, ALU.add).then_inc(nw_done, 1)
                n = 2
                for r in range(3):
                    dve.wait_ge(nw_done, base + n)
                    dve.tensor_tensor(y2, y, y, ALU.mult).then_inc(nw_done, 1)
                    dve.wait_ge(nw_done, base + n + 1)
                    dve.scalar_tensor_tensor(z, y2, -0.5, x, ALU.mult, ALU.mult).then_inc(nw_done, 1)
                    dve.wait_ge(nw_done, base + n + 2)
                    if r == 2:
                        ge(dve, scaled, 4 * (s1 - 1))
                    out = y if r < 2 else rn[par][:, :]
                    dve.scalar_tensor_tensor(out, z, 1.5, y, ALU.add, ALU.mult).then_inc(nw_done if r < 2 else rn_done, 1)
                    n += 3

            def S(u):
                if not live[1]:
                    return
                c = C[u][:, :].rearrange("p (h k) -> p h k", k=64)
                dve.wait_ge(c_ready, 8 * s2 + 5 + u)
                ge(dve, free_c[u], 4 * s2 - 1)
                dve.tensor_reduce(mx[:, 8 * u:8 * u + 8], c, AX.X, ALU.max).then_inc(mx_done, 1)
                dve.wait_ge(mx_done, 2 * s2 + u + 1)
                ge(dve, placed, 160 * (s2 - 1))
                dve.tensor_tensor(E[op][:, 8 * u:8 * u + 8, :], c, mx[:, 8 * u:8 * u + 8].unsqueeze(2).broadcast_to([P, 8, 64]),
                                  ALU.subtract).then_inc(free_c[u], 1)

            def sums():
                if not live[1]:
                    return
                dve.wait_ge(exp_done, 2 * s2 + 2)
                ge(dve, rsum_done, s2)
                dve.tensor_reduce(rs[:, 0, :], E[op][:, :, :], AX.X, ALU.add).then_inc(sum_done, 1)
                dve.wait_ge(sum_done, s2 + 1)
                ge(dve, pn_done, s2)
                dve.reciprocal(rs[:, 1, :], rs[:, 0, :]).then_inc(rsum_done, 1)

            def Y():
                if not live[2]:
                    return
                dve.wait_ge(d_ready, 8 * s3 + 8)
                ge(dve, xb2_done, s3 - 1)
                dve.tensor_tensor(xc[par][:, :], tile_of(X, s3, TILES), Db[1][:, 0:D], ALU.add).then_inc(free_d[1], 1)

            def ln_stats():
                if not live[3]:
                    return
                dve.wait_ge(e_ready, 8 * s4 + 2)
                ge(dve, ln_chain, 3 * s4)
                dve.bn_stats(st[:, :], E4[1][:, 0:P]).then_inc(ln_chain, 1)

            def ln_mean():
                if not live[3]:
                    return
                dve.bn_aggr(mv[:, :], st[:, :]).then_inc(ln_chain, 1)
                dve.wait_ge(ln_chain, 3 * s4 + 2)
                ge(dve, rstd_done, s4)
                dve.tensor_scalar(ve[:, :], mv[:, 1:2], EPS, None, ALU.add).then_inc(ln_chain, 1)

            def ln_apply():
                if not live[3]:
                    return
                dve.wait_ge(rstd_done, s4 + 1)
                ge(dve, e_ready, 8 * (s4 - 1) + 3)
                dve.tensor_scalar(xn[:, :], E4[1][:, 0:P], mv[:, 0:1], rstd[:, 0:1], ALU.subtract, ALU.mult).then_inc(free_e[1], 1)

            def bias1():
                if not live[3]:
                    return
                dve.wait_ge(e_ready, 8 * s4 + 4)
                ge(dve, hm_done, s4)
                dve.tensor_tensor(ha[:, :], E4[1][:, 0:FF], slot(s4, B1_AT, FF), ALU.add).then_inc(free_e[1], 1)
                dve.wait_ge(e_ready, 8 * s4 + 5)
                dve.tensor_tensor(hg[:, :], E4[0][:, 0:FF], slot(s4, B1_AT + FF, FF), ALU.add).then_inc(free_e[0], 1)
                ge(dve, free_e[0], 4 * s4)
                dve.tensor_tensor(xb2[:, :], xc[op][:, :], slot(s4, B2_AT, D), ALU.add).then_inc(xb2_done, 1)

            def gate():
                if not live[3]:
                    return
                dve.wait_ge(gelu_done, s4 + 1)
                ge(dve, e_ready, 8 * (s4 - 1) + 6)
                dve.tensor_tensor(hm[:, 0:FF], ha[:, :], hg[:, :], ALU.mult).then_inc(hm_done, 1)

            def W2():
                if not live[3]:
                    return
                dve.wait_ge(e_ready, 8 * s4 + 7)
                dve.wait_ge(xb2_done, s4 + 1)
                ge(dve, x_kept, s4)
                ge(dve, e_ready, 8 * s4)
                dve.tensor_tensor(x2[:, :], E4[0][:, 0:D], xb2[:, :], ALU.add).then_inc(free_e[0], 1)

            table()
            rotate(0)
            ln_stats()
            rotate(1, after_stats=live[3])
            ln_mean()
            ln_apply()
            S(0)
            rotate(2)
            S(1)
            rotate(3)
            sums()
            bias1()
            gate()
            newton()
            Y()
            W2()

        @block.vector
        def _(dve):
            for l in range(2):
                o = l * SLOT + W2_AT + 2 * D
                m = dve.memset(W[:, o:o + D], 0.0)
            m.then_inc(zeroed, 1)
            for r in range(2):
                dve.memset(qT[r][:, :, :, :, :], 0.0).then_inc(zeroed, 1)
                dve.memset(kT[r][:, :, 0:32], 0.0).then_inc(zeroed, 1)
            for t in (X0f, X1f):
                v = t[64:128, :].rearrange("p (b n) -> p b n", b=B)[:, :, 0:1]
                dve.memset(v, 0.0).then_inc(zeroed, 1)
            dve.memset(hm[:, :], 0.0).then_inc(zeroed, 1)
            dve.memset(mhalf[:, :], -0.5).then_inc(zeroed, 1)
            dve.wait_ge(const_loaded, 32)
            dve.wait_ge(zeroed, 9)
            dve.wait_ge(zeroed_p, 3)
            run(dve_body)(dve)

        def pool_body(pool, i, par, live):
            s1, s2, s3, s4 = i, i - 1, i - 2, i - 3
            op = 1 - par

            def xs1_():
                if not live[3]:
                    return
                pool.wait_ge(free_e[0], 4 * s4 + 1)
                ge(pool, e_ready, 8 * (s4 - 1) + 2)
                pool.tensor_copy(xs1[:, :], cols(X1f, s4)).then_inc(xs1_done, 1)

            def add(c):
                if not live[0]:
                    return
                pool.wait_ge(rot_done, 4 * s1 + c + 1)
                ge(pool, c_ready, 8 * (s1 - 2) + c + 1)
                pool.tensor_tensor(QK[par][:, c, :], t1[c % 2][:, :], t2[c % 2][:, :], ALU.add).then_inc(added, 1)

            def pw():
                if not live[3]:
                    return
                pool.wait_ge(ln_chain, 3 * s4 + 3)
                ge(pool, free_e[1], 3 * s4)
                pool.tensor_tensor(rstd[:, :], ve[:, :], mhalf[:, :], ALU.pow).then_inc(rstd_done, 1)

            def scale(c):
                if not live[0]:
                    return
                pool.wait_ge(rn_done, s1 + 1)
                pool.wait_ge(added, 4 * s1 + c + 1)
                v = QK[par][:, c, :].rearrange("p (h d) -> p h d", d=DH)
                pool.tensor_tensor(v, v, rn[par][:, 8 * c:8 * c + 8].unsqueeze(2).broadcast_to([P, 8, DH]), ALU.mult)\
                    .then_inc(scaled, 1)

            def norm():
                if not live[1]:
                    return
                ge(pool, d_ready, 8 * (s2 - 2) + 6)
                pool.wait_ge(rsum_done, s2 + 1)
                pool.tensor_tensor(E[op][:, :, :], E[op][:, :, :], rs[:, 1, :].unsqueeze(2).broadcast_to([P, 16, 64]), ALU.mult)\
                    .then_inc(pn_done, 1)

            def keep():
                if not live[3]:
                    return
                if live[1]:
                    for r in range(2):
                        pool.wait_ge(free_c[r], 4 * s2 + 4)
                    pool.wait_ge(d_ready, 8 * (s2 - 1) + 7)
                pool.wait_ge(free_e[0], 4 * s4 + 4)
                pool.tensor_copy(tile_of(X, s4, TILES), x2[:, :]).then_inc(x_kept, 1)

            xs1_()
            add(0)
            pw()
            add(1)
            add(2)
            add(3)
            norm()
            if not isinstance(i, int) or i + 1 < STEPS:
                first(pool, i + 1, 1 - par)
            for c in range(4):
                scale(c)
            keep()

        def first(pool, s, par):
            pool.wait_ge(xT_ready, s + 1)
            ge(pool, c_ready, 8 * (s - 2) + 8)
            pool.tensor_copy(xsT[par][:, :], cols(X0f, s)).then_inc(xs_ready, 1)

        @block.gpsimd
        def _(pool):
            for r in range(2):
                m = pool.memset(PA[r][:, :, :], 0.0)
            m.then_inc(zeroed_p, 1)
            for r in range(2):
                pool.memset(Vt[r][:, :, :], 0.0).then_inc(zeroed_p, 1)
            pool.wait_ge(zeroed, 9)
            pool.wait_ge(zeroed_p, 3)
            first(pool, 0, 0)
            run(pool_body)(pool)


def circular_memory(nc, env, w, Z):
    X, ident = env["X"], env["ident"]
    ctx = ExitStack()
    with ctx:
        def sb(name, shape, dt=F32):
            return ctx.enter_context(nc.sbuf_tensor(name, shape, dt))

        def sem(name):
            return ctx.enter_context(nc.semaphore(name))
        bindM = sb("bind_matrix", [P, P])
        unbindM = sb("unbind_matrix", [P, P])
        corrM = sb("corr_matrix", [P, P])
        gate = sb("gate_col", [P, 1])
        dcy = sb("decay_col", [P, 6])
        xT = sb("xT_mem", [P, B * SEQ])
        bound = sb("bound", [P, B * SEQ])
        holo = sb("hologram", [P, B * SEQ])
        bank = [ctx.enter_context(nc.psum_tensor(f"pM{r}", [P, 512], F32)) for r in range(8)]
        spread, loaded, turned, xT_kept, corr_ready, corr_kept = (sem(n) for n in (
            "spread", "loaded", "turned", "xT_kept", "corr_ready", "corr_kept"))
        bound_ready, bound_kept, scanned, out_ready, chain, rooted, summed = (sem(n) for n in (
            "bound_ready", "bound_kept", "scanned", "out_ready", "chain", "powered", "summed"))
        block = ctx.enter_context(nc.Block())

        @block.sync
        def _(sp):
            for k, key in enumerate(("bind", "unbind")):
                rows = w["circulant"][k].rearrange("(p n) -> p n", n=2 * D + 1)
                for half in range(2):
                    sp.dma_start(rows[:, half * D:(half + 1) * D],
                                 w[key].rearrange("(a n) -> a n", a=1).broadcast_to([P, D])).then_inc(spread, 16)
            sp.dma_start(gate[:, :], w["gate"].rearrange("(a n) -> a n", a=1).broadcast_to([P, 1])).then_inc(loaded, 16)
            sp.dma_start(dcy[:, 0:1], w["decay"].rearrange("(a n) -> a n", a=1).broadcast_to([P, 1])).then_inc(loaded, 16)
            sp.wait_ge(spread, 64)
            for k, m in enumerate((bindM, unbindM)):
                src = w["circulant"][k][D:D + 2 * D * (D - 1) + 2 * D].rearrange("(p n) -> p n", n=2 * D)[:, 0:D]
                sp.dma_start(m[:, :], src).then_inc(loaded, 16)

        @block.tensor
        def _(pe):
            for n in range(4):
                for j in range(4):
                    mm = pe.transpose(bank[n][:, j * P:(j + 1) * P], X[:, 4 * n + j, :], ident[:, :])
                mm.then_inc(turned, 1)
            pe.wait_ge(loaded, 64)
            pe.transpose(bank[4][:, 0:P], unbindM[:, :], ident[:, :]).then_inc(corr_ready, 1)
            pe.wait_ge(corr_kept, 1)
            for n in range(4):
                pe.wait_ge(xT_kept, n + 1)
                pe.matmul(bank[4 + n][:, :], bindM[:, :], xT[:, 512 * n:512 * (n + 1)], start=True, stop=True).then_inc(bound_ready, 1)
            for n in range(4):
                pe.wait_ge(scanned, n // 2 + 1)
                for j in range(4):
                    t = 4 * n + j
                    mm = pe.matmul(bank[n][:, j * P:(j + 1) * P], holo[:, t * P:(t + 1) * P], corrM[:, :], start=True, stop=True)
                mm.then_inc(out_ready, 1)

        @block.scalar
        def _(act):
            for n in range(4):
                act.wait_ge(turned, n + 1)
                act.activation(xT[:, 512 * n:512 * (n + 1)], bank[n][:, :], AF.Copy).then_inc(xT_kept, 1)
            act.wait_ge(corr_ready, 1)
            act.activation(corrM[:, :], bank[4][:, 0:P], AF.Copy).then_inc(corr_kept, 1)
            for n in range(4):
                act.wait_ge(bound_ready, n + 1)
                act.activation(bound[:, 512 * n:512 * (n + 1)], bank[4 + n][:, :], AF.Copy).then_inc(bound_kept, 1)

        @block.gpsimd
        def _(pool):
            pool.wait_ge(chain, 2)
            pool.tensor_tensor(dcy[:, 3:4], dcy[:, 2:3], dcy[:, 1:2], ALU.pow).then_inc(rooted, 1)

        @block.vector
        def _(dve):
            dve.wait_ge(loaded, 64)
            dve.tensor_scalar(dcy[:, 1:2], dcy[:, 0:1], -1.0, None, ALU.mult).then_inc(chain, 1)
            dve.memset(dcy[:, 2:3], float(np.e)).then_inc(chain, 1)
            dve.wait_ge(rooted, 1)
            dve.tensor_scalar(dcy[:, 4:5], dcy[:, 3:4], 1.0, None, ALU.add).then_inc(chain, 1)
            dve.wait_ge(chain, 3)
            dve.reciprocal(dcy[:, 5:6], dcy[:, 4:5]).then_inc(chain, 1)
            dve.wait_ge(chain, 4)
            for b in range(B):
                dve.wait_ge(bound_kept, 2 * b + 2)
                t = slice(b * SEQ, (b + 1) * SEQ)
                dve.tensor_tensor_scan(holo[:, t], dcy[:, 5:6].broadcast_to([P, SEQ]), bound[:, t], 0.0, ALU.mult, ALU.add)\
                    .then_inc(scanned, 1)
            for n in range(4):
                t = slice(4 * n, 4 * n + 4)
                dve.wait_ge(out_ready, n + 1)
                dve.scalar_tensor_tensor(Z[:, t, :], bank[n][:, :].rearrange("p (t d) -> p t d", t=4), gate[:, 0:1],
                                         X[:, t, :], ALU.mult, ALU.add).then_inc(summed, 1)
                dve.wait_ge(summed, 2 * n + 1)
                dve.tensor_tensor(Z[:, t, :], Z[:, t, :], X[:, t, :], ALU.add).then_inc(summed, 1)
            dve.wait_ge(summed, 8)


EX, TOPK, FE = 8, 2, 512
NTOK = B * SEQ
CAP = max(1, int(1.25 * NTOK / EX))
FC = FE // P
SLOTS = EX * CAP
BITS = 30
ET = EX * TILES


def routing_constants():
    out = np.zeros((P, 4, ET), np.float32)
    e = np.repeat(np.arange(EX), TILES)
    out[:, 0] = e
    out[:, 1] = e * CAP
    out[:, 2] = np.tile(np.arange(TILES) > 0, EX)
    token = np.arange(TILES)[None, :] * P + np.arange(P)[:, None]
    for k in range(TOPK):
        out[:, 3, k * TILES:(k + 1) * TILES] = SLOTS + k * NTOK + token
    return out


def threshold_bits():
    return np.tile((1 << np.arange(BITS - 1, -1, -1)).astype(np.int32), (P, 1))


def before_matrix():
    return np.stack([np.triu(np.ones((P, P), np.float32), 1), np.ones((P, P), np.float32)], axis=1)


def route(nc, env, w, slots, gathers, weights):
    X, ident = env["X"], env["ident"]
    ctx = ExitStack()
    with ctx:
        def sb(name, shape, dt=F32):
            return ctx.enter_context(nc.sbuf_tensor(name, shape, dt))

        def sem(name):
            return ctx.enter_context(nc.semaphore(name))

        def et(name, dt=F32):
            return sb(name, [P, EX, TILES], dt)
        rw = sb("router_rows", [EX, D])
        rwT = sb("router_turned", [P, EX])
        xT = sb("xT_route", [P, TILES, P])
        cst = sb("route_tab", [P, 4, ET])
        bits = sb("bit_tab", [P, BITS], I32)
        tri = sb("tri_ones", [P, 2, P], BF16)
        zero = sb("zero_rows", [P, SLOTS // P, D])
        Lg, Pr, Pq, oh1, oh2, key, tmp, tmp2, keep, slot = (et(n) for n in (
            "logits", "probs", "probs_rest", "first", "second", "key", "tmp", "tmp2", "keep", "slot"))
        flagb = sb("flags", [P, EX, TILES], BF16)
        flag2 = sb("flags_kept", [P, EX, TILES], BF16)
        cum = sb("cumulated", [P, ET])
        m = sb("token_max", [P, 10, TILES])
        T = sb("threshold", [P, EX])
        cand = sb("candidate", [P, EX])
        cnt = sb("count", [P, 2, EX])
        acc = sb("accepted", [P, EX])
        bank = [ctx.enter_context(nc.psum_tensor(f"pQ{r}", [P, 512], F32)) for r in range(8)]
        loaded, turned, kept, rw_ready, rw_kept, lg_ready, expd = (sem(n) for n in (
            "loaded", "turned", "kept", "rw_ready", "rw_kept", "lg_ready", "expd"))
        chain, flagged, counted, bis, placed, summed, cleared, zeroed, sent = (sem(n) for n in (
            "chain", "flagged", "counted", "bisect", "placed", "summed", "cleared", "zeroed", "sent"))
        block = ctx.enter_context(nc.Block())

        @block.sync
        def _(sp):
            sp.dma_start(rw[:, :], w["router"]).then_inc(loaded, 16)
            sp.dma_start(cst[:, :, :], w["route_consts"]).then_inc(loaded, 16)
            sp.dma_start(bits[:, :], w["bits"]).then_inc(loaded, 16)
            sp.dma_start(tri[:, :, :], w["before"]).then_inc(loaded, 16)
            sp.wait_ge(zeroed, 1)
            sp.dma_start(w["dispatched"][0:SLOTS, :].rearrange("(p n) d -> p n d", p=P), zero[:, :, :]).then_inc(cleared, 16)

        @block.tensor
        def _(pe):
            pe.wait_ge(loaded, 64)
            pe.transpose(bank[4][:, 0:EX], rw[:, :], ident[0:EX, 0:EX]).then_inc(rw_ready, 1)
            for n in range(4):
                for j in range(4):
                    mm = pe.transpose(bank[n][:, j * P:(j + 1) * P], X[:, 4 * n + j, :], ident[:, :])
                mm.then_inc(turned, 1)
            pe.wait_ge(rw_kept, 1)
            for t in range(TILES):
                pe.wait_ge(kept, t // 4 + 1)
                mm = pe.matmul(bank[5][:, t * EX:(t + 1) * EX], xT[:, t, :], rwT[:, :], start=True, stop=True)
            mm.then_inc(lg_ready, 1)

            def count(i):
                pe.wait_ge(flagged, i + 1)
                pe.matmul(bank[6][:, 0:ET], tri[:, 1, :], flagb[:, :, :], start=True, stop=True).then_inc(counted, 1)
            with pe.Fori(0, BITS) as i:
                count(i)
            count(BITS)
            for k, f in enumerate((flagb, flag2)):
                pe.wait_ge(flagged, BITS + 2 + k)
                for j in range(2):
                    mm = pe.matmul(bank[7 - 7 * k][:, j * ET:(j + 1) * ET], tri[:, j, :], f[:, :, :], start=True, stop=True)
                mm.then_inc(summed, 1)

        @block.scalar
        def _(act):
            act.wait_ge(rw_ready, 1)
            act.activation(rwT[:, :], bank[4][:, 0:EX], AF.Copy).then_inc(rw_kept, 1)
            for n in range(4):
                act.wait_ge(turned, n + 1)
                act.activation(xT[:, 4 * n:4 * n + 4, :], bank[n][:, :].rearrange("p (t n) -> p t n", t=4), AF.Copy).then_inc(kept, 1)
            act.wait_ge(chain, 2)
            act.activation(Pr[:, :, :], Lg[:, :, :], AF.Exp).then_inc(expd, 1)

        @block.gpsimd
        def _(pool):
            pool.memset(zero[:, :, :], 0.0).then_inc(zeroed, 1)
            pool.wait_ge(cleared, 16)
            pool.wait_ge(placed, 1)
            for t in range(TILES):
                for k in range(TOPK):
                    pool.indirect_dma_start(out=w["dispatched"], out_offset=bass.IndirectOffsetOnAxis(ap=slots[:, k * TILES + t:k * TILES + t + 1], axis=0),
                                            in_=X[:, t, :], in_offset=None).then_inc(sent, 16)
            pool.wait_ge(sent, 16 * TOPK * TILES)

        @block.vector
        def _(dve):
            n = [0]

            def link(ins):
                n[0] += 1
                ins.then_inc(chain, 1)
                dve.wait_ge(chain, n[0])

            def over_e(t):
                return t[:, :, :].rearrange("p e t -> p t e")

            def wide(v):
                return v.unsqueeze(1).broadcast_to([P, EX, TILES])

            mm_ = [m[:, k, :] for k in range(10)]
            eno = cst[:, 0, :].rearrange("p (e t) -> p e t", e=EX)
            dve.wait_ge(loaded, 64)
            dve.wait_ge(lg_ready, 1)
            lg = bank[5][:, 0:ET].rearrange("p (t e) -> p t e", e=EX)
            link(dve.tensor_reduce(mm_[0], lg, AX.X, ALU.max))
            link(dve.tensor_tensor(Lg[:, :, :], lg.rearrange("p t e -> p e t"), wide(mm_[0]), ALU.subtract))
            dve.wait_ge(expd, 1)
            link(dve.tensor_reduce(mm_[1], over_e(Pr), AX.X, ALU.add))
            link(dve.reciprocal(mm_[2], mm_[1]))
            link(dve.tensor_tensor(Pr[:, :, :], Pr[:, :, :], wide(mm_[2]), ALU.mult))

            def first_max(probs, top, onehot):
                link(dve.tensor_reduce(top, over_e(probs), AX.X, ALU.max))
                link(dve.tensor_tensor(tmp[:, :, :], probs[:, :, :], wide(top), ALU.is_lt))
                link(dve.scalar_tensor_tensor(tmp2[:, :, :], tmp[:, :, :], float(EX), eno, ALU.mult, ALU.add))
                link(dve.tensor_reduce(mm_[9], over_e(tmp2), AX.X, ALU.min))
                link(dve.tensor_tensor(onehot[:, :, :], eno, wide(mm_[9]), ALU.is_equal))
            first_max(Pr, mm_[3], oh1)
            link(dve.scalar_tensor_tensor(Pq[:, :, :], oh1[:, :, :], -4.0, Pr[:, :, :], ALU.mult, ALU.add))
            first_max(Pq, mm_[4], oh2)
            link(dve.tensor_tensor(mm_[5], mm_[3], mm_[4], ALU.add))
            link(dve.tensor_scalar(mm_[5], mm_[5], 1e-6, None, ALU.add))
            link(dve.reciprocal(mm_[6], mm_[5]))
            link(dve.tensor_tensor(mm_[7], mm_[3], mm_[6], ALU.mult))
            link(dve.tensor_tensor(mm_[8], mm_[4], mm_[6], ALU.mult))
            link(dve.tensor_tensor(tmp[:, :, :], oh1[:, :, :], wide(mm_[7]), ALU.mult))
            link(dve.tensor_tensor(tmp2[:, :, :], oh2[:, :, :], wide(mm_[8]), ALU.mult))
            link(dve.tensor_tensor(key[:, :, :], tmp[:, :, :], tmp2[:, :, :], ALU.add))
            link(dve.tensor_tensor(tmp[:, :, :], oh1[:, :, :], oh2[:, :, :], ALU.add))
            link(dve.scalar_tensor_tensor(key[:, :, :], tmp[:, :, :], 1.0, key[:, :, :], ALU.subtract, ALU.add))
            link(dve.memset(T[:, :], 0.0))

            def wide_t(v):
                return v.unsqueeze(2).broadcast_to([P, EX, TILES])

            with dve.Fori(0, BITS) as i:
                dve.tensor_tensor(cand[:, :].bitcast(I32), T[:, :].bitcast(I32), bits[:, bass.ds(i, 1)].broadcast_to([P, EX]),
                                  ALU.bitwise_or).then_inc(bis, 1)
                dve.wait_ge(bis, i * 4 + 1)
                dve.tensor_tensor(flagb[:, :, :], key[:, :, :], wide_t(cand[:, :]), ALU.is_ge).then_inc(flagged, 1)
                dve.wait_ge(counted, i + 1)
                dve.tensor_reduce(cnt[:, 0, :], bank[6][:, 0:ET].rearrange("p (e t) -> p e t", e=EX), AX.X, ALU.add).then_inc(bis, 1)
                dve.wait_ge(bis, i * 4 + 2)
                dve.scalar_tensor_tensor(acc[:, :], cnt[:, 0, :], float(CAP), cand[:, :], ALU.is_ge, ALU.mult).then_inc(bis, 1)
                dve.wait_ge(bis, i * 4 + 3)
                dve.tensor_tensor(T[:, :], T[:, :], acc[:, :], ALU.max).then_inc(bis, 1)
                dve.wait_ge(bis, i * 4 + 4)

            dve.tensor_tensor(flagb[:, :, :], key[:, :, :], wide_t(T[:, :]), ALU.is_gt).then_inc(flagged, 1)
            dve.wait_ge(counted, BITS + 1)
            link(dve.tensor_reduce(cnt[:, 0, :], bank[6][:, 0:ET].rearrange("p (e t) -> p e t", e=EX), AX.X, ALU.add))
            link(dve.tensor_scalar(cnt[:, 1, :], cnt[:, 0, :], -1.0, float(CAP), ALU.mult, ALU.add))
            dve.tensor_tensor(flagb[:, :, :], key[:, :, :], wide_t(T[:, :]), ALU.is_equal).then_inc(flagged, 1)

            def prefix(k, out):
                dve.wait_ge(summed, k + 1)
                tot = bank[7 - 7 * k][:, ET:2 * ET]
                link(dve.tensor_tensor_scan(cum[:, :], cst[:, 2, :], tot, 0.0, ALU.mult, ALU.add))
                link(dve.tensor_tensor(cum[:, :], cum[:, :], tot, ALU.subtract))
                link(dve.tensor_tensor(out[:, :, :].rearrange("p e t -> p (e t)"), cum[:, :], bank[7 - 7 * k][:, 0:ET], ALU.add))
            prefix(0, tmp)
            link(dve.tensor_tensor(tmp2[:, :, :], tmp[:, :, :], wide_t(cnt[:, 1, :]), ALU.is_lt))
            link(dve.tensor_tensor(tmp[:, :, :], key[:, :, :], wide_t(T[:, :]), ALU.is_equal))
            link(dve.tensor_tensor(tmp2[:, :, :], tmp2[:, :, :], tmp[:, :, :], ALU.mult))
            link(dve.tensor_tensor(tmp[:, :, :], key[:, :, :], wide_t(T[:, :]), ALU.is_gt))
            link(dve.tensor_tensor(keep[:, :, :], tmp[:, :, :], tmp2[:, :, :], ALU.add))
            dve.tensor_copy(flag2[:, :, :], keep[:, :, :]).then_inc(flagged, 1)
            prefix(1, slot)
            link(dve.tensor_tensor(slot[:, :, :], slot[:, :, :], cst[:, 1, :].rearrange("p (e t) -> p e t", e=EX), ALU.add))
            link(dve.tensor_tensor(slot[:, :, :], slot[:, :, :], keep[:, :, :], ALU.mult))
            for k, (oh, wt) in enumerate(((oh1, mm_[7]), (oh2, mm_[8]))):
                c = slice(k * TILES, (k + 1) * TILES)
                link(dve.tensor_tensor(tmp[:, :, :], oh[:, :, :], slot[:, :, :], ALU.mult))
                link(dve.tensor_reduce(mm_[0], over_e(tmp), AX.X, ALU.add))
                link(dve.tensor_tensor(tmp[:, :, :], oh[:, :, :], keep[:, :, :], ALU.mult))
                link(dve.tensor_reduce(mm_[1], over_e(tmp), AX.X, ALU.add))
                link(dve.tensor_tensor(weights[:, c], wt, mm_[1], ALU.mult))
                link(dve.tensor_copy(gathers[:, c], mm_[0]))
                link(dve.tensor_scalar(mm_[1], mm_[1], -1.0, 1.0, ALU.mult, ALU.add))
                link(dve.tensor_tensor(mm_[1], mm_[1], cst[:, 3, c], ALU.mult))
                link(dve.tensor_tensor(mm_[2], mm_[0], mm_[1], ALU.add))
                dve.wait_ge(chain, n[0])
                ins = dve.tensor_copy(slots[:, c], mm_[2])
                if k == 0:
                    link(ins)
                else:
                    ins.then_inc(placed, 1)
            dve.wait_ge(placed, 1)


def experts(nc, env, w):
    ident = env["ident"]
    PARTIAL = CAP % P
    CT = -(-CAP // P)
    ctx = ExitStack()
    with ctx:
        def sb(name, shape, dt=F32):
            return ctx.enter_context(nc.sbuf_tensor(name, shape, dt))

        def sem(name):
            return ctx.enter_context(nc.semaphore(name))
        WG = [sb(f"w_gate{r}", [P, FE]) for r in range(2)]
        WU = [sb(f"w_up{r}", [P, FE]) for r in range(2)]
        WD = [sb(f"w_down{r}", [P, FC, D]) for r in range(2)]
        xe = [sb(f"x_expert{r}", [P, CT, D]) for r in range(2)]
        xeT = [sb(f"xT_expert{r}", [P, CAP]) for r in range(2)]
        sg = [sb(f"silu{r}", [P, CAP]) for r in range(2)]
        hT = [sb(f"hT{r}", [P, FC, CAP]) for r in range(2)]
        yo = [sb(f"y_expert{r}", [P, CT, D]) for r in range(2)]
        G = [ctx.enter_context(nc.psum_tensor(f"pG{r}", [P, 512], F32)) for r in range(2)]
        U = [ctx.enter_context(nc.psum_tensor(f"pU{r}", [P, 512], F32)) for r in range(2)]
        XT = [ctx.enter_context(nc.psum_tensor(f"pX{r}", [P, 512], F32)) for r in range(2)]
        Y = [ctx.enter_context(nc.psum_tensor(f"pYe{r}", [P, 512], F32)) for r in range(2)]
        loaded = [sem(f"expert_loaded{r}") for r in range(2)]
        xt_ready, xt_kept = sem("xt_ready"), sem("xt_kept")
        gu_ready, silu_done, h_done = sem("gu_ready"), sem("silu_done"), sem("h_done")
        y_ready, y_kept = sem("y_ready"), sem("y_kept")
        stored = [sem(f"expert_stored{r}") for r in range(2)]
        block = ctx.enter_context(nc.Block())
        rows = [(c, min(P, CAP - c * P)) for c in range(CT)]

        @block.sync
        def _(sp):
            for e in range(EX):
                r = e % 2
                if e >= 2:
                    sp.wait_ge(y_ready, e - 1)
                sp.dma_start(WG[r][:, :], w["wg"][e]).then_inc(loaded[r], 16)
                sp.dma_start(WU[r][:, :], w["wu"][e]).then_inc(loaded[r], 16)
                sp.dma_start(WD[r][:, :, :], w["wd"][e].rearrange("(c p) n -> p c n", p=P)).then_inc(loaded[r], 16)
                at = e * CAP
                sp.dma_start(xe[r][:, 0:CAP // P, :], w["dispatched"][at:at + CAP - PARTIAL, :].rearrange("(c p) d -> p c d", p=P))\
                    .then_inc(loaded[r], 16)
                sp.dma_start(xe[r][0:PARTIAL, CT - 1, :], w["dispatched"][at + CAP - PARTIAL:at + CAP, :]).then_inc(loaded[r], 16)

        @block.tensor
        def _(pe):
            def turn(e):
                r = e % 2
                pe.wait_ge(loaded[r], 80 * (e // 2 + 1))
                if e >= 2:
                    pe.wait_ge(xt_kept, e - 1)
                for c, k in rows:
                    mm = pe.transpose(XT[r][:, c * P:c * P + k], xe[r][0:k, c, :], ident[0:k, 0:k])
                mm.then_inc(xt_ready, 1)

            def up(e):
                r = e % 2
                pe.wait_ge(xt_kept, e + 1)
                for f in range(FC):
                    n = FC * e + f
                    if n >= 2:
                        pe.wait_ge(h_done, n - 1)
                    pe.matmul(G[n % 2][:, 0:CAP], WG[r][:, f * P:(f + 1) * P], xeT[r][:, :], start=True, stop=True)
                    pe.matmul(U[n % 2][:, 0:CAP], WU[r][:, f * P:(f + 1) * P], xeT[r][:, :], start=True, stop=True).then_inc(gu_ready, 1)

            def down(e):
                r = e % 2
                pe.wait_ge(h_done, FC * (e + 1))
                if e >= 2:
                    pe.wait_ge(y_kept, e - 1)
                for c, k in rows:
                    for f in range(FC):
                        mm = pe.matmul(Y[r][0:k, c * P:(c + 1) * P], hT[r][:, f, c * P:c * P + k], WD[r][:, f, :],
                                       start=(f == 0), stop=(f == FC - 1), skip_group_check=True)
                mm.then_inc(y_ready, 1)
            turn(0)
            for e in range(EX):
                up(e)
                if e + 1 < EX:
                    turn(e + 1)
                down(e)

        @block.scalar
        def _(act):
            def keep(e):
                act.wait_ge(xt_ready, e + 1)
                if e >= 2:
                    act.wait_ge(gu_ready, FC * (e - 1))
                act.activation(xeT[e % 2][:, :], XT[e % 2][:, 0:CAP], AF.Copy).then_inc(xt_kept, 1)

            keep(0)
            for e in range(EX):
                for f in range(FC):
                    n = FC * e + f
                    act.wait_ge(gu_ready, n + 1)
                    if n >= 2:
                        act.wait_ge(h_done, n - 1)
                    act.activation(sg[n % 2][:, :], G[n % 2][:, 0:CAP], AF.Silu).then_inc(silu_done, 1)
                if e + 1 < EX:
                    keep(e + 1)
                act.wait_ge(y_ready, e + 1)
                if e >= 2:
                    act.wait_ge(stored[e % 2], 32 * (e // 2))
                act.activation(yo[e % 2][0:PARTIAL, CT - 1, :], Y[e % 2][0:PARTIAL, (CT - 1) * P:CT * P], AF.Copy)
                act.activation(yo[e % 2][:, 0:CT - 1, :], Y[e % 2][:, 0:(CT - 1) * P].rearrange("p (c d) -> p c d", c=CT - 1), AF.Copy)\
                    .then_inc(y_kept, 1)

        @block.vector
        def _(dve):
            for n in range(FC * EX):
                e, f = divmod(n, FC)
                dve.wait_ge(silu_done, n + 1)
                if e >= 2:
                    dve.wait_ge(y_ready, e - 1)
                dve.tensor_tensor(hT[e % 2][:, f, :], sg[n % 2][:, :], U[n % 2][:, 0:CAP], ALU.mult).then_inc(h_done, 1)

        @block.gpsimd
        def _(pool):
            for e in range(EX):
                at = e * CAP
                pool.wait_ge(y_kept, e + 1)
                pool.dma_start(w["expert_out"][at:at + CAP - PARTIAL, :].rearrange("(c p) d -> p c d", p=P), yo[e % 2][:, 0:CT - 1, :])\
                    .then_inc(stored[e % 2], 16)
                pool.dma_start(w["expert_out"][at + CAP - PARTIAL:at + CAP, :], yo[e % 2][0:PARTIAL, CT - 1, :])\
                    .then_inc(stored[e % 2], 16)
            for r in range(2):
                pool.wait_ge(stored[r], 32 * (EX // 2))


def combine(nc, env, w, gathers, weights, Z):
    X = env["X"]
    RING = 4
    ctx = ExitStack()
    with ctx:
        got = [[ctx.enter_context(nc.sbuf_tensor(f"gathered{k}{r}", [P, D], F32)) for r in range(RING)] for k in range(TOPK)]
        arrived = [ctx.enter_context(nc.semaphore(f"arrived{r}")) for r in range(RING)]
        added = ctx.enter_context(nc.semaphore("added"))
        block = ctx.enter_context(nc.Block())

        @block.gpsimd
        def _(pool):
            for t in range(TILES):
                if t >= RING:
                    pool.wait_ge(added, 2 * (t - RING + 1))
                for k in range(TOPK):
                    pool.indirect_dma_start(out=got[k][t % RING][:, :], out_offset=None, in_=w["expert_out"],
                                            in_offset=bass.IndirectOffsetOnAxis(ap=gathers[:, k * TILES + t:k * TILES + t + 1], axis=0))\
                        .then_inc(arrived[t % RING], 16)

        @block.vector
        def _(dve):
            for t in range(TILES):
                dve.wait_ge(arrived[t % RING], 32 * (t // RING + 1))
                for k in range(TOPK):
                    c = k * TILES + t
                    dve.scalar_tensor_tensor(Z[:, t, :], got[k][t % RING][:, :], weights[:, c:c + 1],
                                             (X if k == 0 else Z)[:, t, :], ALU.mult, ALU.add).then_inc(added, 1)
                    dve.wait_ge(added, 2 * t + k + 1)


def load_tokens(nc, w, X, ident, identb):
    ctx = ExitStack()
    with ctx:
        loaded = ctx.enter_context(nc.semaphore("x_loaded"))
        cast = ctx.enter_context(nc.semaphore("ident_cast"))
        block = ctx.enter_context(nc.Block())

        @block.sync
        def _(sp):
            sp.dma_start(ident[:, :], w["identity"]).then_inc(loaded, 16)
            sp.dma_start(X[:, :, :], w["x"].rearrange("(t p) d -> p t d", p=P)).then_inc(loaded, 16)
            sp.wait_ge(loaded, 32)

        @block.vector
        def _(dve):
            dve.wait_ge(loaded, 32)
            dve.tensor_copy(identb[:, :], ident[:, :]).then_inc(cast, 1)
            dve.wait_ge(cast, 1)


def set_aside(nc, w, X):
    ctx = ExitStack()
    with ctx:
        copied = ctx.enter_context(nc.semaphore("copied"))
        block = ctx.enter_context(nc.Block())

        @block.sync
        def _(sp):
            sp.dma_start(w["aside"], X[:, :, :]).then_inc(copied, 16)
            sp.wait_ge(copied, 16)


def add_aside(nc, w, X, Z, T):
    ctx = ExitStack()
    with ctx:
        loaded = ctx.enter_context(nc.semaphore("aside_loaded"))
        summed = ctx.enter_context(nc.semaphore("residual_summed"))
        block = ctx.enter_context(nc.Block())

        @block.sync
        def _(sp):
            sp.dma_start(T[:, :, :], w["aside"]).then_inc(loaded, 16)

        @block.vector
        def _(dve):
            dve.wait_ge(loaded, 16)
            dve.tensor_tensor(Z[:, :, :], T[:, :, :], X[:, :, :], ALU.add).then_inc(summed, 1)
            dve.wait_ge(summed, 1)


def store_tokens(nc, w, X):
    ctx = ExitStack()
    with ctx:
        stored = ctx.enter_context(nc.semaphore("result_stored"))
        block = ctx.enter_context(nc.Block())

        @block.sync
        def _(sp):
            sp.dma_start(w["result"].rearrange("(t p) d -> p t d", p=P), X[:, :, :]).then_inc(stored, 16)
            sp.wait_ge(stored, 16)


def program(nc, w):
    w = dict(w)
    for name, shape, dt in (("stacked", (2, PARTS, P, B * SEQ), BF16), ("maxima", (PARTS * GH * SEQ,), BF16),
                            ("aside", (P, TILES, D), F32), ("circulant", (2, D * (2 * D + 1)), F32),
                            ("dispatched", (SLOTS + TOPK * NTOK, D), F32), ("expert_out", (SLOTS, D), F32)):
        w[name] = nc.dram_tensor(name, shape, dt, kind="Internal").ap()
    ctx = ExitStack()
    with ctx:
        def tokens(scope, name):
            return scope.enter_context(nc.sbuf_tensor(name, [P, TILES, D], F32))
        X = tokens(ctx, "tokens")
        ident = ctx.enter_context(nc.sbuf_tensor("ident", [P, P], F32))
        identb = ctx.enter_context(nc.sbuf_tensor("ident_bf16", [P, P], BF16))
        env = {"X": X, "ident": ident, "identb": identb}
        load_tokens(nc, w, X, ident, identb)
        with ExitStack() as scope:
            V, O, Z = (tokens(scope, n) for n in ("values", "attended", "summed_a"))
            project_heads(nc, env, w, V)
            causal_attention(nc, env, w, V, O)
            project_out(nc, env, w, O, Z)
            layernorm_all(nc, Z, X, V, "norm_a")
        set_aside(nc, w, X)
        window_layers(nc, env, w)
        with ExitStack() as scope:
            Z, T = tokens(scope, "summed_b"), tokens(scope, "squares_b")
            add_aside(nc, w, X, Z, T)
            layernorm_all(nc, Z, X, T, "norm_b")
        with ExitStack() as scope:
            Z, T = tokens(scope, "summed_c"), tokens(scope, "squares_c")
            circular_memory(nc, env, w, Z)
            layernorm_all(nc, Z, X, T, "norm_c")
            slots = scope.enter_context(nc.sbuf_tensor("slots", [P, TOPK * TILES], mybir.dt.uint32))
            gathers = scope.enter_context(nc.sbuf_tensor("gathers", [P, TOPK * TILES], mybir.dt.uint32))
            weights = scope.enter_context(nc.sbuf_tensor("route_weights", [P, TOPK * TILES], F32))
            route(nc, env, w, slots, gathers, weights)
            experts(nc, env, w)
            combine(nc, env, w, gathers, weights, Z)
            layernorm_all(nc, Z, X, T, "norm_d")
        store_tokens(nc, w, X)


_INS = {"L0_attn_x": "x", "L0_attn_w_qkv": "a_w_qkv", "L0_attn_b_qkv": "a_b_qkv", "L0_attn_w_out": "a_w_out",
        "L0_attn_b_out": "a_b_out", "L0_ffn_Wqkv": "Wqkv", "L0_ffn_q_scale": "q_scale", "L0_ffn_k_scale": "k_scale",
        "L0_ffn_Wo": "Wo", "L0_ffn_ln_g": "ln_g", "L0_ffn_ln_b": "ln_b", "L0_ffn_W1": "W1", "L0_ffn_b1": "b1",
        "L0_ffn_W2": "W2", "L0_ffn_b2": "b2", "L1_attn_bind_key": "bind", "L1_attn_unbind_key": "unbind",
        "L1_attn_gate": "gate", "L1_attn_decay": "decay", "L1_ffn_router_w": "router", "L1_ffn_wg": "wg",
        "L1_ffn_wu": "wu", "L1_ffn_wd": "wd"}


def kernel(**inputs):
    import numpy as _np
    import concourse.bacc as _bacc
    from concourse import mybir as _mybir
    from concourse.bass_utils import run_bass_kernel_spmd as _run

    def high_half(a):
        return (a.view(_np.uint32) >> 16).astype(_np.uint16)

    nc = _bacc.Bacc("TRN2", target_bir_lowering=False, num_devices=1)
    given = {short: _np.ascontiguousarray(inputs[name]) for name, short in _INS.items()}
    given["x"] = given["x"].reshape(B * SEQ, D)
    given["decay"] = given["decay"].reshape(1)
    given.update(identity=_np.eye(P, dtype=_np.float32), rope=rope_tables(), xpos=xpos_tables(),
                 route_consts=routing_constants(), bits=threshold_bits())
    halves = {"causal": causal_masks(), "mask": window_mask(), "before": before_matrix()}
    arrays, w = {}, {}
    for name, a in [*given.items(), *((n, high_half(a)) for n, a in halves.items())]:
        a = _np.ascontiguousarray(a)
        arrays[f"in_{name}_dram"] = a
        ap = nc.dram_tensor(f"in_{name}_dram", a.shape, _mybir.dt.from_np(a.dtype), kind="ExternalInput").ap()
        w[name] = ap.bitcast(BF16) if name in halves else ap
    w["result"] = nc.dram_tensor("out_0_dram", (B * SEQ, D), _mybir.dt.float32, kind="ExternalOutput").ap()
    program(nc, w)
    r = _run(nc, [arrays], core_ids=[0])
    return r.results[0]["out_0_dram"].reshape(B, SEQ, D)
```
